# Optimizing a Trainium2 kernel written in Bass

```python
import numpy as np
import jax
import jax.numpy as jnp

def _softmax(x, axis=-1):
    return jax.nn.softmax(x, axis=axis)

def _gelu(x):
    return jax.nn.gelu(x, approximate=True)

def _silu(x):
    return jax.nn.silu(x)

def _sigmoid(x):
    return jax.nn.sigmoid(x)

def _layernorm(x, axis=-1, eps=1e-05):
    m = jnp.mean(x, axis=axis, keepdims=True)
    v = jnp.var(x, axis=axis, keepdims=True)
    return (x - m) / jnp.sqrt(v + eps)

def _scatter_add(tgt, idx, src, axis=0):
    return tgt.at[idx].add(src)

def _segment_sum(src, seg, n):
    return jax.ops.segment_sum(src, seg, n)
kernel_name = 'mk_audio_tower_d1_tok_audfeat512_r4_3cecf3'

def setup_inputs(seed: int=0):
    np.random.seed(seed)
    _w = jnp.asarray

    def _rec_inputs():
        import jax
        import jax.numpy as jnp
        _rk = jax.random.key(seed)
        x = 7.22013e-05 + 1.00017 * jax.random.normal(jax.random.fold_in(_rk, 1), (64, 750, 32), jnp.float32)
        return x
    x = _rec_inputs()

    def _L0_tok_setup():
        import jax, jax.numpy as jnp
        import numpy as np
        PATCH_LEN = 16
        STRIDE = 8
        D_MODEL = 128
        N_FEATURES = 32
        key = jax.random.key(seed)
        k1, k2 = jax.random.split(key)
        x = jax.random.normal(k1, (64, 1024, N_FEATURES), dtype=jnp.float32)
        fan_in = PATCH_LEN * N_FEATURES
        W = jax.random.normal(k2, (D_MODEL, fan_in), dtype=jnp.float32) / np.sqrt(fan_in)
        b = jnp.zeros((D_MODEL,), dtype=jnp.float32)
        return {'x': x, 'W': W, 'b': b}
    _L0_tok_all = _L0_tok_setup()
    _L0_tok_in = {k: v for k, v in _L0_tok_all.items() if k in ('W', 'b')}
    del _L0_tok_all

    def _L0_attn_setup():
        import jax, jax.numpy as jnp
        import numpy as np
        D_MODEL = 128
        NUM_HEADS = 8
        D_K = D_MODEL // NUM_HEADS
        key = jax.random.key(seed)
        ks = jax.random.split(key, 9)
        B, S = (4, 512)
        s = 1.0 / np.sqrt(D_MODEL)
        inp = {'x': jax.random.normal(ks[0], (B, S, D_MODEL), dtype=jnp.float32), 'Wq': jax.random.uniform(ks[1], (D_MODEL, D_MODEL), jnp.float32, -s, s), 'bq': jax.random.uniform(ks[2], (D_MODEL,), jnp.float32, -s, s), 'Wk': jax.random.uniform(ks[3], (D_MODEL, D_MODEL), jnp.float32, -s, s), 'bk': jax.random.uniform(ks[4], (D_MODEL,), jnp.float32, -s, s), 'Wv': jax.random.uniform(ks[5], (D_MODEL, D_MODEL), jnp.float32, -s, s), 'bv': jax.random.uniform(ks[6], (D_MODEL,), jnp.float32, -s, s), 'Wo': jax.random.uniform(ks[7], (D_MODEL, D_MODEL), jnp.float32, -s, s), 'bo': jax.random.uniform(ks[8], (D_MODEL,), jnp.float32, -s, s)}
        return inp
    _L0_attn_all = _L0_attn_setup()
    _L0_attn_in = {k: v for k, v in _L0_attn_all.items() if k in ('Wq', 'bq', 'Wk', 'bk', 'Wv', 'bv', 'Wo', 'bo')}
    del _L0_attn_all

    def _L0_ffn_setup():
        import jax, jax.numpy as jnp
        import numpy as np
        N_DIM = 128
        HEADS = 8
        NUM_EXPERTS = 16384
        NUM_KEYS = 64
        DIM_KEY = 64
        TOPK = 16
        SCALE = 0.02
        key = jax.random.key(seed)
        k0, k1, k2, k3, k4 = jax.random.split(key, 5)
        x = jax.random.normal(k0, (1, 512, N_DIM), dtype=jnp.float32)
        W_q = jax.random.normal(k1, (N_DIM, 2 * HEADS * DIM_KEY), dtype=jnp.float32) * SCALE
        keys = jax.random.normal(k2, (HEADS, NUM_KEYS, 2, DIM_KEY), dtype=jnp.float32) * SCALE
        down_embed = jax.random.normal(k3, (NUM_EXPERTS, N_DIM), dtype=jnp.float32) * SCALE
        up_embed = jax.random.normal(k4, (NUM_EXPERTS, N_DIM), dtype=jnp.float32) * SCALE
        return {'x': x, 'W_q': W_q, 'keys': keys, 'down_embed': down_embed, 'up_embed': up_embed}
    _L0_ffn_all = _L0_ffn_setup()
    _L0_ffn_in = {k: v for k, v in _L0_ffn_all.items() if k in ('W_q', 'keys', 'down_embed', 'up_embed')}
    del _L0_ffn_all
    return {'x': x, 'L0_tok_W': _L0_tok_in['W'], 'L0_tok_b': _L0_tok_in['b'], 'L0_attn_Wq': _L0_attn_in['Wq'], 'L0_attn_bq': _L0_attn_in['bq'], 'L0_attn_Wk': _L0_attn_in['Wk'], 'L0_attn_bk': _L0_attn_in['bk'], 'L0_attn_Wv': _L0_attn_in['Wv'], 'L0_attn_bv': _L0_attn_in['bv'], 'L0_attn_Wo': _L0_attn_in['Wo'], 'L0_attn_bo': _L0_attn_in['bo'], 'L0_ffn_W_q': _L0_ffn_in['W_q'], 'L0_ffn_keys': _L0_ffn_in['keys'], 'L0_ffn_down_embed': _L0_ffn_in['down_embed'], 'L0_ffn_up_embed': _L0_ffn_in['up_embed']}

def reference(x, L0_tok_W, L0_tok_b, L0_attn_Wq, L0_attn_bq, L0_attn_Wk, L0_attn_bk, L0_attn_Wv, L0_attn_bv, L0_attn_Wo, L0_attn_bo, L0_ffn_W_q, L0_ffn_keys, L0_ffn_down_embed, L0_ffn_up_embed):
    import jax
    import jax.numpy as jnp

    def _L0_tok_ref(x, W, b):
        import jax, jax.numpy as jnp
        import numpy as np
        PATCH_LEN = 16
        STRIDE = 8
        D_MODEL = 128
        N_FEATURES = 32
        batch, seq_len, n_feat = x.shape
        starts = jnp.arange(0, seq_len - PATCH_LEN + 1, STRIDE)
        idx = starts[:, None] + jnp.arange(PATCH_LEN)[None, :]
        patches = x[:, idx, :]
        n_patches = starts.shape[0]
        patches = patches.reshape(batch, n_patches, PATCH_LEN * n_feat)
        return jnp.einsum('bpf,df->bpd', patches, W) + b

    def _L0_attn_ref(x, Wq, bq, Wk, bk, Wv, bv, Wo, bo):
        import jax, jax.numpy as jnp
        import numpy as np
        D_MODEL = 128
        NUM_HEADS = 8
        D_K = D_MODEL // NUM_HEADS
        B, S, _ = x.shape

        def heads(t):
            return t.reshape(B, S, NUM_HEADS, D_K).transpose(0, 2, 1, 3)
        Q = heads(x @ Wq + bq)
        K = heads(x @ Wk + bk)
        V = heads(x @ Wv + bv)
        scale = 1.0 / jnp.sqrt(jnp.asarray(D_K, dtype=x.dtype))
        scores = jnp.einsum('bhqd,bhkd->bhqk', Q, K) * scale
        attn = jax.nn.softmax(scores, axis=-1)
        ctx = jnp.einsum('bhqk,bhkd->bhqd', attn, V)
        ctx = ctx.transpose(0, 2, 1, 3).reshape(B, S, D_MODEL)
        return ctx @ Wo + bo

    def _L0_ffn_ref(x, W_q, keys, down_embed, up_embed):
        import jax, jax.numpy as jnp
        import numpy as np
        N_DIM = 128
        HEADS = 8
        NUM_EXPERTS = 16384
        NUM_KEYS = 64
        DIM_KEY = 64
        TOPK = 16
        SCALE = 0.02
        b, n, d = x.shape
        q = (x @ W_q).reshape(b, n, 2, HEADS, DIM_KEY).transpose(2, 0, 1, 3, 4)
        sim = jnp.einsum('pbnhd,hkpd->pbnhk', q, keys)
        sx, ix = jax.lax.top_k(sim[0], TOPK)
        sy, iy = jax.lax.top_k(sim[1], TOPK)
        all_scores = (sx[..., :, None] + sy[..., None, :]).reshape(b, n, HEADS, TOPK * TOPK)
        scores, pk_idx = jax.lax.top_k(all_scores, TOPK)
        w_down = down_embed[pk_idx]
        w_up = up_embed[pk_idx]
        h = jnp.einsum('bnd,bnhkd->bnhk', x, w_down)
        h = jax.nn.gelu(h, approximate=False)
        h = jax.nn.softmax(scores, axis=-1) * h
        return jnp.einsum('bnhk,bnhkd->bnd', h, w_up)
    h = _L0_tok_ref(x, L0_tok_W, L0_tok_b)
    h = h + _L0_attn_ref(_layernorm(h, axis=-1), L0_attn_Wq, L0_attn_bq, L0_attn_Wk, L0_attn_bk, L0_attn_Wv, L0_attn_bv, L0_attn_Wo, L0_attn_bo)
    h = h + _L0_ffn_ref(_layernorm(h, axis=-1), L0_ffn_W_q, L0_ffn_keys, L0_ffn_down_embed, L0_ffn_up_embed)
    return h

_drawn_inputs = setup_inputs


def setup_inputs(seed=0):
    import zlib

    import numpy as np

    out = dict(_drawn_inputs(seed))
    spreads = {'L0_tok_b': (0.0, 0.1)}
    factors = {'L0_attn_Wq': 3.628,
     'L0_attn_bq': 8.0,
     'L0_attn_Wk': 3.64,
     'L0_attn_bk': 8.0,
     'L0_ffn_W_q': 8.0,
     'L0_ffn_keys': 8.0,
     'L0_ffn_down_embed': 8.0,
     'L0_ffn_up_embed': 8.0}
    for name, (base, spread) in spreads.items():
        noise = np.random.default_rng([zlib.crc32(name.encode()), seed]).standard_normal(out[name].shape)
        drawn = base * np.exp(spread * noise) if base else spread * noise
        out[name] = jnp.asarray(drawn.astype(out[name].dtype))
    for name, factor in factors.items():
        out[name] = (out[name] * factor).astype(out[name].dtype)
    return out
```

```python
from contextlib import ExitStack

import concourse.bass as bass
from concourse import mybir

F32 = mybir.dt.float32
ALU = mybir.AluOpType
ACT = mybir.ActivationFunctionType
AX_X = mybir.AxisListType.X

BATCH, SEQ, FEAT = 64, 750, 32
PATCH, STRIDE = 16, 8
DM = 128
NP = (SEQ - PATCH) // STRIDE + 1
NSEG = NP + 1
NCH = PATCH * FEAT // 128
HEADS, DK = 8, 16
KEYS, DKEY, TOPK = 64, 64, 16
EPS = 1e-5

GB = 4
NG = BATCH // GB
COLS = GB * NP
TILES = 3
T0 = [0, 128, COLS - 128]
SKIP = [0, 0, 2 * 128 - (COLS - 128)]

ROW = [TOPK // (i + 1) for i in range(TOPK)]
PAIRS = [i * TOPK + j for i in range(TOPK) for j in range(ROW[i])]
NC = len(PAIRS)
ROW0 = [sum(ROW[:i]) for i in range(TOPK)]
RUNS = []
for i in range(TOPK):
    if RUNS and RUNS[-1][2] == ROW[i]:
        RUNS[-1] = (RUNS[-1][0], RUNS[-1][1] + 1, ROW[i])
    else:
        RUNS.append((i, 1, ROW[i]))

NSIM = 2 * HEADS * KEYS
SIMW = NSIM + NC
SCH = 3
CW = SIMW // SCH
TAKEN = -2.0 ** 126

C_TOK, C_ATT, C_ID, C_CEN, C_DOWN = 0, 512, 1024, 1152, 1280
C_COL = C_DOWN + NC
C_END = C_COL + 7
COL_B, COL_BQ, COL_BK, COL_BV, COL_BO, COL_ME, COL_MO = range(7)


def wait(eng, sem, value):
    if not (isinstance(value, int) and value <= 0):
        eng.wait_ge(sem, value)


def build(nc, x, wpack, qkpack, up, out):
    out_rows = out.rearrange("b p d -> (b p) d")

    with ExitStack() as ctx:
        def sb(name, shape):
            return ctx.enter_context(nc.sbuf_tensor(name, shape, F32))

        def bank(name):
            return ctx.enter_context(nc.psum_tensor(name, [128, 512], F32))

        def sem(name):
            return ctx.enter_context(nc.semaphore(name))

        w_tok = sb("w_tok", [128, NCH, DM])
        w_att = sb("w_att", [128, 4, DM])
        ident = sb("ident", [128, 128])
        center = sb("center", [128, 128])
        cols = sb("cols", [128, 7])
        w_sim = sb("w_sim", [128, SIMW])
        qk = sb("qk", [64, 2 * HEADS * (DM + KEYS)])
        w_up = sb("w_up", [128, DM])
        bq_even = sb("bq_even", [128, 1])
        bq_odd = sb("bq_odd", [128, 1])
        bo_all = sb("bo_all", [128, 1])
        xT = sb("xT", [128, GB, 2, NSEG])
        hT = sb("hT", [128, COLS])
        hR = sb("hR", [128, COLS])
        hc = sb("hc", [NP, GB, DM])
        ss = sb("ss", [NP, GB])
        var = sb("var", [NP, GB])
        rstd = sb("rstd", [NP, GB])
        junk = sb("junk", [128, 2, GB, DM])
        power = sb("power", [128, GB])
        xn = sb("xn", [NP, GB, DM])
        xnT = sb("xnT", [128, COLS])
        q_even = sb("q_even", [128, COLS])
        q_odd = sb("q_odd", [128, COLS])
        kT = sb("kT", [128, COLS])
        vx = sb("vx", [NP, GB, HEADS, 32])
        negm = sb("negm", [NP, 8, 4])
        probs = [sb(f"probs{i}", [NP, 4, NP]) for i in range(2)]
        probsT = [sb(f"probsT{i}", [NP, 4, NP]) for i in range(2)]
        cu = sb("cu", [128, 2, COLS])
        rl = sb("rl", [NP, 16])
        ctx_tok = sb("ctx_tok", [NP, GB, DM])
        ctxT = sb("ctxT", [128, COLS])
        h2T = sb("h2T", [128, COLS])
        hc2 = sb("hc2", [128, TILES, DM])
        ss2 = sb("ss2", [128, TILES])
        var2 = sb("var2", [128, TILES])
        rstd2 = sb("rstd2", [128, TILES])
        xn2 = sb("xn2", [128, TILES, DM])
        xn2T = sb("xn2T", [128, TILES, 128])
        h2R = sb("h2R", [128, COLS])
        sims = sb("sims", [128, TILES, SIMW])
        best = sb("best", [128, TILES, 2, HEADS, TOPK])
        cand = sb("cand", [128, TILES, HEADS, NC])
        left = sb("left", [128, TILES, HEADS, NC])
        top = sb("top", [128, TILES, HEADS, TOPK])
        shifted = sb("shifted", [128, TILES, HEADS * (NC + TOPK)])
        expd = sb("expd", [128, TILES, HEADS * (NC + TOPK)])
        taken = sb("taken", [128, TILES, HEADS, NC])
        den = sb("den", [128, TILES, HEADS])
        rden = sb("rden", [128, TILES, HEADS])
        wsel = sb("wsel", [128, HEADS, NC])
        wnorm = sb("wnorm", [128, HEADS, NC])
        wsum4 = sb("wsum4", [128, 4, NC])
        wsum2 = sb("wsum2", [128, 2, NC])
        wsum1 = sb("wsum1", [128, NC])
        gel = sb("gel", [128, TILES, NC])
        u = sb("u", [128, TILES, 128])
        uT = sb("uT", [128, 128])
        out_sb = sb("out_sb", [128, TILES, DM])

        W0, W1, S0, S1, PT, CT, F0, F1 = [bank(f"ps{i}") for i in range(8)]
        S = [S0, S1]
        FB = [F0, F1]

        dve_passed, pool_passed = sem("dve_passed"), sem("pool_passed")
        consts_loaded = sem("consts_loaded")
        filled = sem("filled")
        wsim_ps = sem("wsim_ps")
        wsim_ready = sem("wsim_ready")
        bo_ps = sem("bo_ps")
        x_loaded = sem("x_loaded")
        tok_ps = sem("tok_ps")
        hT_ready = sem("hT_ready")
        hc_ps = sem("hc_ps")
        hc_ready = sem("hc_ready")
        ln1 = sem("ln1")
        xn_ready = sem("xn_ready")
        xnT_ps = sem("xnT_ps")
        xnT_ready = sem("xnT_ready")
        q_ps, k_ps, v_ps = sem("q_ps"), sem("k_ps"), sem("v_ps")
        q_ready, k_ready, v_ready = sem("q_ready"), sem("k_ready"), sem("v_ready")
        hR_ready = sem("hR_ready")
        s_ps = sem("s_ps")
        max_ready = sem("max_ready")
        exp_ready = sem("exp_ready")
        pT_ps = sem("pT_ps")
        pT_ready = sem("pT_ready")
        pv_ps = sem("pv_ps")
        cu_ready = sem("cu_ready")
        cuT_ps = sem("cuT_ps")
        rl_ready = sem("rl_ready")
        ctx_ready = sem("ctx_ready")
        ctxT_ps, ctxT_ready = sem("ctxT_ps"), sem("ctxT_ready")
        h2_ps, h2T_ready = sem("h2_ps"), sem("h2T_ready")
        hc2_ps, hc2_ready = sem("hc2_ps"), sem("hc2_ready")
        ln2 = sem("ln2")
        xn2_ready = sem("xn2_ready")
        xn2T_ps, xn2T_ready = sem("xn2T_ps"), sem("xn2T_ready")
        sim_ps, sim_ready = sem("sim_ps"), sem("sim_ready")
        best_done = sem("best_done")
        cand_ready = sem("cand_ready")
        top_done = sem("top_done")
        gel_ready = sem("gel_ready")
        h2R_ready = sem("h2R_ready")
        shifted_ready = sem("shifted_ready")
        weights_exp = sem("weights_exp")
        den_ready, rden_ready = sem("den_ready"), sem("rden_ready")
        wchain = sem("wchain")
        u_ready = sem("u_ready")
        uT_ps, uT_ready = sem("uT_ps"), sem("uT_ready")
        out_ps, out_ready = sem("out_ps"), sem("out_ready")
        stored = [sem(f"stored{t}") for t in range(TILES)]

        N_CONST = 16 * 8

        def steps(eng, front, step):
            front(0)
            step(0, attn=True, ffn=False, late=False, nxt=True)
            step(1, attn=True, ffn=True, late=False, nxt=True)
            step(2, attn=True, ffn=True, late=True, nxt=True)
            with eng.Fori(3, NG - 1) as g:
                step(g, attn=True, ffn=True, late=True, nxt=True)
            step(NG - 1, attn=True, ffn=True, late=True, nxt=False)
            step(NG, attn=False, ffn=True, late=True, nxt=False)
            step(NG + 1, attn=False, ffn=False, late=True, nxt=False)

        def own_wait(eng, passed):
            eng.sem_inc(passed, 1)

        block = ctx.enter_context(nc.Block())

        @block.sync
        def _(sp):
            sp.dma_start(w_tok[:], wpack[:, C_TOK:C_ATT].rearrange("p (c d) -> p c d", c=NCH)).then_inc(consts_loaded, 16)
            sp.dma_start(cols[:], wpack[:, C_COL:C_END]).then_inc(consts_loaded, 16)
            sp.dma_start(xT[:], x[0]).then_inc(x_loaded, 16)
            sp.dma_start(ident[:], wpack[:, C_ID:C_CEN]).then_inc(consts_loaded, 16)
            sp.dma_start(center[:], wpack[:, C_CEN:C_DOWN]).then_inc(consts_loaded, 16)
            sp.dma_start(w_att[:], wpack[:, C_ATT:C_ID].rearrange("p (c d) -> p c d", c=4)).then_inc(consts_loaded, 16)
            sp.dma_start(w_sim[:, NSIM:SIMW], wpack[:, C_DOWN:C_COL]).then_inc(consts_loaded, 16)
            sp.dma_start(qk[:], qkpack).then_inc(consts_loaded, 16)
            sp.wait_ge(filled, 1)
            sp.dma_start(w_up[0:NC, :], up).then_inc(consts_loaded, 16)

            def step(g, attn, ffn, late, nxt):
                e = g - 2
                if nxt:
                    sp.wait_ge(tok_ps, g + 1)
                    sp.dma_start(xT[:], x[g + 1]).then_inc(x_loaded, 16)
                if late:
                    for t in range(TILES):
                        sp.wait_ge(out_ready, TILES * e + t + 1)
                        row = COLS * e + T0[t] + SKIP[t]
                        sp.dma_start(out_rows[bass.ds(row, 128 - SKIP[t]), :],
                                     out_sb[SKIP[t]:128, t, :]).then_inc(stored[t], 16)

            steps(sp, lambda g: None, step)
            for t in range(TILES):
                sp.wait_ge(stored[t], 16 * NG)

        @block.tensor
        def _(pe):
            mm, tr = nc.tensor.matmul, nc.tensor.transpose

            def front_tok(g):
                pe.wait_ge(x_loaded, 16 * (g + 1))
                wait(pe, q_ready, g)
                wait(pe, out_ready, TILES * (g - 2))
                for c in range(NCH):
                    last = mm(W0[:, 0:COLS], w_tok[:, c, :], xT[:, :, c % 2, c // 2:c // 2 + NP],
                              start=(c == 0), stop=(c == NCH - 1))
                last.then_inc(tok_ps, 1)

            def front_center(g):
                pe.wait_ge(hT_ready, g + 1)
                for b in range(GB):
                    last = mm(W0[0:NP, b * DM:(b + 1) * DM], hT[:, b * NP:(b + 1) * NP], center[:],
                              start=True, stop=True)
                last.then_inc(hc_ps, 1)

            def front_xnT(g):
                pe.wait_ge(xn_ready, g + 1)
                for b in range(GB):
                    last = tr(W0[:, b * NP:(b + 1) * NP], xn[:, b, :], ident[0:NP, 0:NP])
                last.then_inc(xnT_ps, 1)

            def front_q(g):
                pe.wait_ge(xnT_ready, g + 1)
                mm(W0[:, 0:COLS], w_att[:, 0, :], xnT[:], start=True, stop=True).then_inc(q_ps, 1)

            def front_k(g):
                wait(pe, exp_ready, 8 * g)
                mm(S0[:, 0:COLS], w_att[:, 1, :], xnT[:], start=True, stop=True).then_inc(k_ps, 1)

            def front_v(g):
                for b in range(GB):
                    last = mm(S1[0:NP, b * DM:(b + 1) * DM], xnT[:, b * NP:(b + 1) * NP],
                              w_att[:, 2, :], start=True, stop=True)
                last.then_inc(v_ps, 1)

            def scores(g, n):
                pair, strip = n // 4, n % 4
                if n == 0:
                    pe.wait_ge(q_ready, g + 1)
                    pe.wait_ge(k_ready, g + 1)
                if n == 1:
                    pe.wait_ge(v_ready, g + 1)
                if n >= 2:
                    pe.wait_ge(exp_ready, 8 * g + n - 1)
                r = 32 * strip
                for j in range(4):
                    b, q = 2 * pair + j // 2, (q_even, q_odd)[j % 2]
                    last = mm(S[n % 2][0:NP, j * NP:(j + 1) * NP], q[r:r + 32, b * NP:(b + 1) * NP],
                              kT[r:r + 32, b * NP:(b + 1) * NP], start=True, stop=True)
                last.then_inc(s_ps, 1)

            def probs_T(g, n):
                pe.wait_ge(exp_ready, 8 * g + n + 1)
                wait(pe, pT_ready, 8 * g + n)
                for j in range(4):
                    last = tr(PT[0:NP, j * NP:(j + 1) * NP], probs[n % 2][:, j, :], ident[0:NP, 0:NP])
                last.then_inc(pT_ps, 1)

            def values(g, n):
                pair, strip = n // 4, n % 4
                pe.wait_ge(pT_ready, 8 * g + n + 1)
                if n % 4 == 0:
                    wait(pe, cu_ready, 2 * g + n // 4)
                for j in range(4):
                    b, h = j // 2, 2 * strip + j % 2
                    at = (2 * b + h // 4) * NP
                    last = mm(CT[32 * (h % 4):32 * (h % 4) + 32, at:at + NP], vx[:, 2 * pair + b, h, :],
                              probsT[n % 2][:, j, :], start=True, stop=True)
                last.then_inc(pv_ps, 1)

            def ctx_back(g, pair):
                pe.wait_ge(cu_ready, 2 * g + pair + 1)
                if pair == 0:
                    wait(pe, xn2T_ready, g)
                else:
                    pe.wait_ge(ctx_ready, 2 * g + 1)
                for i in range(4):
                    last = tr(W1[0:NP, i * 128:(i + 1) * 128], cu[:, pair, i * NP:(i + 1) * NP], ident[:])
                last.then_inc(cuT_ps, 1)

            def tail_ctxT(g):
                pe.wait_ge(ctx_ready, 2 * g + 2)
                for b in range(GB):
                    last = tr(W1[:, b * NP:(b + 1) * NP], ctx_tok[:, b, :], ident[0:NP, 0:NP])
                last.then_inc(ctxT_ps, 1)

            def tail_h2(g):
                pe.wait_ge(ctxT_ready, g + 1)
                pe.wait_ge(hR_ready, g + 1)
                mm(W1[:, 0:COLS], w_att[:, 3, :], ctxT[:], start=True, stop=False)
                mm(W1[:, 0:COLS], ident[:], hR[:], start=False, stop=True).then_inc(h2_ps, 1)

            def tail_center(g):
                pe.wait_ge(h2T_ready, g + 1)
                for t in range(TILES):
                    last = mm(W1[:, t * 128:(t + 1) * 128], h2T[:, T0[t]:T0[t] + 128], center[:],
                              start=True, stop=True)
                last.then_inc(hc2_ps, 1)

            def tail_xn2T(g):
                pe.wait_ge(xn2_ready, g + 1)
                for t in range(TILES):
                    last = tr(W1[:, t * 128:(t + 1) * 128], xn2[:, t, :], ident[:])
                last.then_inc(xn2T_ps, 1)

            def sim(f, t, k):
                c = SCH * t + k
                if c == 0:
                    pe.wait_ge(xn2T_ready, f + 1)
                wait(pe, sim_ready, 9 * f + max(c - 1, 0))
                mm(FB[c % 2][:, 0:CW], xn2T[:, t, :], w_sim[:, k * CW:(k + 1) * CW],
                   start=True, stop=True).then_inc(sim_ps, 1)

            def late_uT(e, t):
                pe.wait_ge(u_ready, TILES * e + t + 1)
                if t == 0:
                    pe.wait_ge(q_ready, min(e + 3, NG) if isinstance(e, int) else e + 3)
                else:
                    pe.wait_ge(out_ready, TILES * e + t)
                tr(W0[:, 0:128], u[:, t, :], ident[:]).then_inc(uT_ps, 1)

            def late_out(e, t):
                pe.wait_ge(uT_ready, TILES * e + t + 1)
                pe.wait_ge(h2R_ready, e + 1)
                mm(W0[:, 128:256], uT[:], w_up[:], start=True, stop=False)
                mm(W0[:, 128:256], h2R[:, T0[t]:T0[t] + 128], ident[:], start=False, stop=True).then_inc(out_ps, 1)

            pe.wait_ge(consts_loaded, N_CONST)
            for i in range(2 * HEADS):
                last = mm(FB[i // HEADS][:, (i % HEADS) * KEYS:(i % HEADS + 1) * KEYS],
                          qk[:, i * DM:(i + 1) * DM],
                          qk[:, 2 * HEADS * DM + i * KEYS:2 * HEADS * DM + (i + 1) * KEYS],
                          start=True, stop=True)
                if i % HEADS == HEADS - 1:
                    last.then_inc(wsim_ps, 1)
            mm(CT[:, 0:1], w_att[:, 3, :], cols[:, COL_BV:COL_BV + 1], start=True, stop=True).then_inc(bo_ps, 1)
            pe.wait_ge(filled, 5)
            pe.wait_ge(wsim_ready, 3)

            def front(g):
                front_tok(g)
                front_center(g)
                front_xnT(g)
                front_q(g)
                front_k(g)
                front_v(g)

            def step(g, attn, ffn, late, nxt):
                f, e = g - 1, g - 2
                fill = [[] for _ in range(8)]
                if ffn:
                    for k in range(SCH):
                        fill[k].append(lambda k=k: sim(f, 1, k))
                        fill[k + 4].append(lambda k=k: sim(f, 2, k))
                if late:
                    for t in range(TILES):
                        fill[2 * t + 1].append(lambda t=t: late_uT(e, t))
                        fill[2 * t + 2].append(lambda t=t: late_out(e, t))
                if attn:
                    fill[6].append(lambda: ctx_back(g, 0))
                    scores(g, 0)
                    scores(g, 1)
                if ffn:
                    for k in range(SCH):
                        sim(f, 0, k)
                for n in range(8):
                    if attn:
                        if n + 2 < 8:
                            scores(g, n + 2)
                        probs_T(g, n)
                        if n >= 1:
                            values(g, n - 1)
                    for part in fill[n]:
                        part()
                if attn:
                    values(g, 7)
                    if nxt:
                        front_tok(g + 1)
                    ctx_back(g, 1)
                    if nxt:
                        front_center(g + 1)
                    tail_ctxT(g)
                    if nxt:
                        front_xnT(g + 1)
                    tail_h2(g)
                    if nxt:
                        front_q(g + 1)
                        front_k(g + 1)
                    tail_center(g)
                    if nxt:
                        front_v(g + 1)
                    tail_xn2T(g)

            steps(pe, front, step)

        @block.scalar
        def _(act):
            run = nc.scalar.activation

            def bias(i):
                return cols[:, i:i + 1]

            def front_hT(g):
                act.wait_ge(tok_ps, g + 1)
                wait(act, hR_ready, g)
                run(hT[:], W0[:, 0:COLS], ACT.Identity, bias=bias(COL_B)).then_inc(hT_ready, 1)

            def front_hc(g):
                act.wait_ge(hc_ps, g + 1)
                run(hc[:], W0[0:NP, :].rearrange("p (b d) -> p b d", b=GB), ACT.Copy)
                for b in range(GB):
                    last = run(junk[0:NP, 0, b, :], W0[0:NP, b * DM:(b + 1) * DM], ACT.Square,
                               accum_out=ss[:, b:b + 1])
                last.then_inc(hc_ready, 1)

            def front_xnT(g):
                act.wait_ge(xnT_ps, g + 1)
                run(xnT[:], W0[:, 0:COLS], ACT.Copy).then_inc(xnT_ready, 1)

            def front_q(g):
                act.wait_ge(q_ps, g + 1)
                run(q_even[:], W0[:, 0:COLS], ACT.Identity, bias=bq_even[:], scale=bias(COL_ME))
                run(q_odd[:], W0[:, 0:COLS], ACT.Identity, bias=bq_odd[:], scale=bias(COL_MO)).then_inc(q_ready, 1)

            def front_k(g):
                act.wait_ge(k_ps, g + 1)
                run(kT[:], S0[:, 0:COLS], ACT.Identity, bias=bias(COL_BK)).then_inc(k_ready, 1)

            def front_v(g):
                act.wait_ge(v_ps, g + 1)
                run(vx[:, :, :, 0:DK], S1[0:NP, :].rearrange("p (b h d) -> p b h d", b=GB, h=HEADS),
                    ACT.Copy).then_inc(v_ready, 1)

            def exps(g, n):
                act.wait_ge(max_ready, 8 * g + n + 1)
                wait(act, pT_ps, 8 * g + n - 1)
                for j in range(4):
                    last = run(probs[n % 2][:, j, :], S[n % 2][0:NP, j * NP:(j + 1) * NP], ACT.Exp,
                               bias=negm[:, n, j:j + 1])
                last.then_inc(exp_ready, 1)

            def copy_pT(g, n):
                act.wait_ge(pT_ps, 8 * g + n + 1)
                wait(act, pv_ps, 8 * g + n - 1)
                run(probsT[n % 2][:], PT[0:NP, 0:COLS].rearrange("p (j q) -> p j q", j=4),
                    ACT.Copy).then_inc(pT_ready, 1)

            def copy_cu(g, pair):
                act.wait_ge(pv_ps, 8 * g + 4 * pair + 4)
                run(cu[:, pair, :], CT[:, 0:COLS], ACT.Copy).then_inc(cu_ready, 1)

            def tail_ctxT(g):
                act.wait_ge(ctxT_ps, g + 1)
                run(ctxT[:], W1[:, 0:COLS], ACT.Copy).then_inc(ctxT_ready, 1)

            def tail_h2(g):
                act.wait_ge(h2_ps, g + 1)
                wait(act, h2R_ready, g)
                run(h2T[:], W1[:, 0:COLS], ACT.Identity, bias=bo_all[:]).then_inc(h2T_ready, 1)

            def tail_hc(g):
                act.wait_ge(hc2_ps, g + 1)
                run(hc2[:], W1[:, 0:TILES * DM].rearrange("p (t d) -> p t d", t=TILES), ACT.Copy)
                for t in range(TILES):
                    last = run(junk[:, 1, t, :], W1[:, t * DM:(t + 1) * DM], ACT.Square, accum_out=ss2[:, t:t + 1])
                last.then_inc(hc2_ready, 1)

            def tail_xn2T(g):
                act.wait_ge(xn2T_ps, g + 1)
                run(xn2T[:], W1[:, 0:TILES * 128].rearrange("p (t d) -> p t d", t=TILES),
                    ACT.Copy).then_inc(xn2T_ready, 1)

            def copy_sim(f, t, k):
                c = SCH * t + k
                act.wait_ge(sim_ps, 9 * f + c + 1)
                if k == 0:
                    wait(act, best_done, 18 * (f - 1) + 6 * t + 6)
                run(sims[:, t, k * CW:(k + 1) * CW], FB[c % 2][:, 0:CW], ACT.Copy).then_inc(sim_ready, 1)

            def gelu(f):
                act.wait_ge(sim_ready, 9 * f + 9)
                wait(act, u_ready, TILES * f)
                run(gel[:], sims[:, :, NSIM:SIMW], ACT.Gelu).then_inc(gel_ready, 1)

            def late_exp(e, t):
                act.wait_ge(shifted_ready, TILES * e + t + 1)
                wait(act, u_ready, TILES * e)
                run(expd[:, t, :], shifted[:, t, :], ACT.Exp)
                run(taken[:, t, :, :], left[:, t, :, :], ACT.Relu, scale=1.0 / TAKEN,
                    ).then_inc(weights_exp, 1)

            def late_uT(e, t):
                act.wait_ge(uT_ps, TILES * e + t + 1)
                run(uT[:], W0[:, 0:128], ACT.Copy).then_inc(uT_ready, 1)

            def late_out(e, t):
                act.wait_ge(out_ps, TILES * e + t + 1)
                wait(act, stored[t], 16 * e)
                run(out_sb[:, t, :], W0[:, 128:256], ACT.Copy).then_inc(out_ready, 1)

            for i in range(2):
                act.wait_ge(wsim_ps, i + 1)
                run(w_sim[:, i * 512:(i + 1) * 512], FB[i][:], ACT.Copy).then_inc(wsim_ready, 1)
            act.wait_ge(bo_ps, 1)
            run(bo_all[:], CT[:, 0:1], ACT.Identity, bias=bias(COL_BO)).then_inc(wsim_ready, 1)
            act.wait_ge(filled, 5)

            def front(g):
                front_hT(g)
                front_hc(g)
                front_xnT(g)
                front_q(g)
                front_k(g)
                front_v(g)

            def step(g, attn, ffn, late, nxt):
                f, e = g - 1, g - 2
                fill = [[] for _ in range(8)]
                if late:
                    for t in range(TILES):
                        fill[t].append(lambda t=t: late_exp(e, t))
                        fill[2 * t + 1].append(lambda t=t: late_uT(e, t))
                        fill[2 * t + 2].append(lambda t=t: late_out(e, t))
                if ffn:
                    for k in range(SCH):
                        fill[k].append(lambda k=k: copy_sim(f, 1, k))
                        fill[k + 4].append(lambda k=k: copy_sim(f, 2, k))
                        copy_sim(f, 0, k)
                    fill[7].append(lambda: gelu(f))
                if attn:
                    fill[5].insert(0, lambda: copy_cu(g, 0))
                for n in range(8):
                    if attn:
                        exps(g, n)
                        if n >= 1:
                            copy_pT(g, n - 1)
                    for part in fill[n]:
                        part()
                if attn:
                    copy_pT(g, 7)
                    if nxt:
                        front_hT(g + 1)
                    copy_cu(g, 1)
                    if nxt:
                        front_hc(g + 1)
                    tail_ctxT(g)
                    if nxt:
                        front_xnT(g + 1)
                    tail_h2(g)
                    if nxt:
                        front_q(g + 1)
                        front_k(g + 1)
                    tail_hc(g)
                    if nxt:
                        front_v(g + 1)
                    tail_xn2T(g)

            steps(act, front, step)

        @block.vector
        def _(dve):
            def first_topk(f, t, i):
                p, rnd = i % 2, i // 2
                base = 18 * f + 6 * t
                if i == 0:
                    dve.wait_ge(sim_ready, 9 * f + SCH * t + 3)
                    wait(dve, cand_ready, TILES * (f - 1) + t + 1)
                if rnd:
                    dve.wait_ge(best_done, base + i - 1)
                own_wait(dve, dve_passed)
                for h in range(HEADS):
                    at = (p * HEADS + h) * KEYS
                    src = sims[:, t, at:at + KEYS]
                    if rnd == 0:
                        last = dve.max(best[:, t, p, h, 0:8], src)
                    elif rnd == 1:
                        last = dve.match_replace(out=src, in_to_replace=best[:, t, p, h, 0:8],
                                                 in_values=src, imm_value=TAKEN)
                    else:
                        last = dve.max(best[:, t, p, h, 8:16], src)
                last.then_inc(best_done, 1)

            def second_topk(f, t, i):
                rnd = i // 2
                base = 24 * f + 8 * t
                if i == 0:
                    dve.wait_ge(cand_ready, TILES * f + t + 1)
                    wait(dve, shifted_ready, TILES * (f - 1) + t + 1)
                    wait(dve, weights_exp, TILES * (f - 1) + t + 1)
                if rnd:
                    dve.wait_ge(top_done, base + i - 1)
                own_wait(dve, dve_passed)
                for h in range(4 * (i % 2), 4 * (i % 2) + 4):
                    if rnd == 0:
                        last = dve.max(top[:, t, h, 0:8], cand[:, t, h, :])
                    elif rnd == 1:
                        last = dve.match_replace(out=left[:, t, h, :], in_to_replace=top[:, t, h, 0:8],
                                                 in_values=cand[:, t, h, :], imm_value=TAKEN)
                    elif rnd == 2:
                        last = dve.max(top[:, t, h, 8:16], left[:, t, h, :])
                    else:
                        last = dve.match_replace(out=left[:, t, h, :], in_to_replace=top[:, t, h, 8:16],
                                                 in_values=left[:, t, h, :], imm_value=TAKEN)
                last.then_inc(top_done, 1)

            def row_max(g, n):
                dve.wait_ge(s_ps, 8 * g + n + 1)
                dve.tensor_reduce(negm[:, n, :], S[n % 2][0:NP, 0:COLS].rearrange("p (j k) -> p j k", j=4),
                                  AX_X, ALU.max, negate=True).then_inc(max_ready, 1)

            def normalise(g, pair):
                dve.wait_ge(cuT_ps, 2 * g + pair + 1)
                src = W1[0:NP, :].rearrange("p (i c) -> p i c", c=32)
                dve.reciprocal(rl[:], src[:, :, DK]).then_inc(rl_ready, 1)
                dve.wait_ge(rl_ready, 2 * g + pair + 1)
                dst = ctx_tok[:, 2 * pair:2 * pair + 2, :].rearrange("p b (h d) -> p (b h) d", d=DK)
                dve.tensor_tensor(dst, src[:, :, 0:DK], rl[:].unsqueeze(2).to_broadcast([NP, 16, DK]),
                                  ALU.mult).then_inc(ctx_ready, 1)

            def denominator(e, t):
                dve.wait_ge(weights_exp, TILES * e + t + 1)
                wait(dve, u_ready, TILES * e)
                dve.tensor_reduce(den[:, t, :], expd[:, t, HEADS * NC:].rearrange("p (h k) -> p h k", h=HEADS),
                                  AX_X, ALU.add).then_inc(den_ready, 1)
                dve.wait_ge(den_ready, TILES * e + t + 1)
                dve.reciprocal(rden[:, t, :], den[:, t, :]).then_inc(rden_ready, 1)

            dve.memset(w_up[:], 0.0).then_inc(filled, 1)
            dve.memset(vx[:], 0.0).then_inc(filled, 1)
            dve.memset(u[:], 0.0)
            dve.memset(power[:], -0.5).then_inc(filled, 1)
            dve.wait_ge(filled, 3)
            dve.memset(vx[:, :, :, DK:DK + 1], 1.0).then_inc(filled, 1)
            dve.wait_ge(consts_loaded, N_CONST)
            dve.tensor_tensor(bq_even[:], cols[:, COL_BQ:COL_BQ + 1], cols[:, COL_ME:COL_ME + 1], ALU.mult)
            dve.tensor_tensor(bq_odd[:], cols[:, COL_BQ:COL_BQ + 1], cols[:, COL_MO:COL_MO + 1],
                              ALU.mult).then_inc(filled, 1)

            def step(g, attn, ffn, late, nxt):
                f, e = g - 1, g - 2
                work = [lambda i=i: second_topk(e, 2, i) if late else None for i in range(8)]
                for what, t, k in ((first_topk, 0, 6), (first_topk, 1, 6), (second_topk, 0, 8),
                                   (first_topk, 2, 6), (second_topk, 1, 8)):
                    work += [lambda what=what, t=t, i=i: what(f, t, i) if ffn else None for i in range(k)]
                also = {}
                if attn:
                    for n, at in enumerate((1, 6, 9, 11, 13, 15, 17, 21)):
                        also.setdefault(at, []).append(lambda n=n: row_max(g, n))
                    also.setdefault(24, []).append(lambda: normalise(g, 0))
                    also.setdefault(29, []).append(lambda: normalise(g, 1))
                if late:
                    for t, at in enumerate((8, 12, 16)):
                        also.setdefault(at, []).append(lambda t=t: denominator(e, t))
                for i, part in enumerate(work):
                    part()
                    for other in also.get(i, []):
                        other()

            steps(dve, lambda g: None, step)

        @block.gpsimd
        def _(pool):
            tt, ts = nc.gpsimd.tensor_tensor, nc.gpsimd.tensor_scalar

            def layernorm(ready, chain, done, g, squares, v, r, src, dst, n):
                pool.wait_ge(ready, g + 1)
                own_wait(pool, pool_passed)
                ts(v[:], squares[:], 1.0 / DM, EPS, ALU.mult, ALU.add).then_inc(chain, 1)
                pool.wait_ge(chain, 2 * g + 1)
                tt(r[:], v[:], power[0:v.shape[0], 0:n], ALU.pow).then_inc(chain, 1)
                pool.wait_ge(chain, 2 * g + 2)
                tt(dst[:], src[:], r[:].unsqueeze(2).to_broadcast([v.shape[0], n, DM]), ALU.mult).then_inc(done, 1)

            def front_ln(g):
                layernorm(hc_ready, ln1, xn_ready, g, ss, var, rstd, hc, xn, GB)

            def tail_ln(g):
                layernorm(hc2_ready, ln2, xn2_ready, g, ss2, var2, rstd2, hc2, xn2, TILES)

            def save_h(g):
                pool.wait_ge(hT_ready, g + 1)
                wait(pool, h2_ps, g)
                own_wait(pool, pool_passed)
                nc.gpsimd.tensor_copy(hR[:], hT[:]).then_inc(hR_ready, 1)

            def save_h2(f, late):
                pool.wait_ge(h2T_ready, f + 1)
                if late:
                    wait(pool, out_ps, TILES * f)
                own_wait(pool, pool_passed)
                nc.gpsimd.tensor_copy(h2R[:], h2T[:]).then_inc(h2R_ready, 1)

            def sums(f, t):
                pool.wait_ge(best_done, 18 * f + 6 * t + 6)
                wait(pool, top_done, 24 * (f - 1) + 8 * t + 8)
                for i, n, w in RUNS:
                    dst = cand[:, t, :, ROW0[i]:ROW0[i] + n * w].rearrange("p h (n w) -> p h n w", n=n)
                    sx = best[:, t, 0, :, i:i + n].unsqueeze(3).to_broadcast([128, HEADS, n, w])
                    sy = best[:, t, 1, :, 0:w].unsqueeze(2).to_broadcast([128, HEADS, n, w])
                    last = tt(dst, sx, sy, ALU.add)
                last.then_inc(cand_ready, 1)

            def shift(e, t):
                pool.wait_ge(top_done, 24 * e + 8 * t + 8)
                wait(pool, weights_exp, TILES * e)
                tt(shifted[:, t, 0:HEADS * NC].rearrange("p (h c) -> p h c", h=HEADS), cand[:, t, :, :],
                   top[:, t, :, 0:1].to_broadcast([128, HEADS, NC]), ALU.subtract)
                tt(shifted[:, t, HEADS * NC:].rearrange("p (h c) -> p h c", h=HEADS), top[:, t, :, :],
                   top[:, t, :, 0:1].to_broadcast([128, HEADS, TOPK]), ALU.subtract).then_inc(shifted_ready, 1)

            def weigh(e, t):
                base = 5 * (TILES * e + t)
                pool.wait_ge(weights_exp, TILES * e + t + 1)
                tt(wsel[:], expd[:, t, 0:HEADS * NC].rearrange("p (h c) -> p h c", h=HEADS),
                   taken[:, t, :, :], ALU.mult).then_inc(wchain, 1)
                pool.wait_ge(wchain, base + 1)
                pool.wait_ge(rden_ready, TILES * e + t + 1)
                tt(wnorm[:], wsel[:], rden[:, t, :].unsqueeze(2).to_broadcast([128, HEADS, NC]),
                   ALU.mult).then_inc(wchain, 1)
                pool.wait_ge(wchain, base + 2)
                tt(wsum4[:], wnorm[:, 0:4, :], wnorm[:, 4:8, :], ALU.add).then_inc(wchain, 1)
                pool.wait_ge(wchain, base + 3)
                tt(wsum2[:], wsum4[:, 0:2, :], wsum4[:, 2:4, :], ALU.add).then_inc(wchain, 1)
                pool.wait_ge(wchain, base + 4)
                tt(wsum1[:], wsum2[:, 0, :], wsum2[:, 1, :], ALU.add).then_inc(wchain, 1)
                pool.wait_ge(wchain, base + 5)
                pool.wait_ge(gel_ready, e + 1)
                wait(pool, uT_ps, TILES * e)
                tt(u[:, t, 0:NC], wsum1[:], gel[:, t, :], ALU.mult).then_inc(u_ready, 1)

            pool.wait_ge(filled, 5)

            def step(g, attn, ffn, late, nxt):
                f, e = g - 1, g - 2
                if attn:
                    save_h(g)
                if late:
                    shift(e, 0)
                    shift(e, 1)
                    weigh(e, 0)
                    shift(e, 2)
                    weigh(e, 1)
                if ffn:
                    sums(f, 0)
                if late:
                    weigh(e, 2)
                if ffn:
                    save_h2(f, late)
                    sums(f, 1)
                if nxt:
                    front_ln(g + 1)
                if attn:
                    tail_ln(g)
                if ffn:
                    sums(f, 2)

            steps(pool, front_ln, step)


def kernel(x, L0_tok_W, L0_tok_b, L0_attn_Wq, L0_attn_bq, L0_attn_Wk, L0_attn_bk, L0_attn_Wv, L0_attn_bv,
           L0_attn_Wo, L0_attn_bo, L0_ffn_W_q, L0_ffn_keys, L0_ffn_down_embed, L0_ffn_up_embed):
    import numpy as np
    import concourse.bacc as bacc
    from concourse.bass_utils import run_bass_kernel_spmd

    segs = np.asarray(x)[:, :NSEG * STRIDE, :].reshape(NG, GB, NSEG, 2, 128)
    x_dev = np.ascontiguousarray(segs.transpose(0, 4, 1, 3, 2))

    tokW = np.asarray(L0_tok_W).T.reshape(NCH, 128, DM).transpose(1, 0, 2).reshape(128, NCH * DM)
    row = np.arange(128)
    even = (row // DK % 2 == 0).astype(np.float32) * DK ** -0.5
    odd = (row // DK % 2 == 1).astype(np.float32) * DK ** -0.5
    ident = np.eye(128, dtype=np.float32)
    center = (np.eye(DM) - 1.0 / DM).astype(np.float32)
    down = np.asarray(L0_ffn_down_embed)[PAIRS].T
    columns = [np.asarray(v)[:, None] for v in (L0_tok_b, L0_attn_bq, L0_attn_bk, L0_attn_bv, L0_attn_bo, even, odd)]
    wpack = np.ascontiguousarray(np.concatenate(
        [tokW, np.asarray(L0_attn_Wq), np.asarray(L0_attn_Wk), np.asarray(L0_attn_Wv), np.asarray(L0_attn_Wo),
         ident, center, down, *columns], axis=1))

    wq = np.asarray(L0_ffn_W_q).reshape(DM, 2 * HEADS, DKEY).transpose(2, 1, 0).reshape(DKEY, -1)
    keys = np.asarray(L0_ffn_keys).transpose(3, 2, 0, 1).reshape(DKEY, -1)
    qkpack = np.ascontiguousarray(np.concatenate([wq, keys], axis=1))
    up = np.ascontiguousarray(np.asarray(L0_ffn_up_embed)[PAIRS])

    nc = bacc.Bacc("TRN2", target_bir_lowering=False, num_devices=1)
    arrays = {"x_dram": x_dev, "wpack_dram": wpack, "qkpack_dram": qkpack, "up_dram": up}
    args = [nc.dram_tensor(name, a.shape, F32, kind="ExternalInput").ap() for name, a in arrays.items()]
    out = nc.dram_tensor("out_0_dram", (BATCH, NP, DM), F32, kind="ExternalOutput").ap()
    build(nc, *args, out)
    r = run_bass_kernel_spmd(nc, [arrays], core_ids=[0])
    return r.results[0]["out_0_dram"]
```

```python
from contextlib import ExitStack

import concourse.bass as bass
from concourse import mybir

F32 = mybir.dt.float32
ALU = mybir.AluOpType
ACT = mybir.ActivationFunctionType
AX_X = mybir.AxisListType.X

BATCH, SEQ, FEAT = 64, 750, 32
PATCH, STRIDE = 16, 8
DM = 128
NP = (SEQ - PATCH) // STRIDE + 1
NSEG = NP + 1
NCH = PATCH * FEAT // 128
HEADS, DK = 8, 16
KEYS, DKEY, TOPK = 64, 64, 16
EPS = 1e-5

GB = 4
NG = BATCH // GB
COLS = GB * NP
TILES = 3
T0 = [0, 128, COLS - 128]
SKIP = [0, 0, 2 * 128 - (COLS - 128)]

def staircase(k):
    row = [k // (i + 1) for i in range(k)]
    start = [sum(row[:i]) for i in range(k)]
    runs = []
    for i in range(k):
        if runs and runs[-1][2] == row[i]:
            runs[-1] = (runs[-1][0], runs[-1][1] + 1, row[i])
        else:
            runs.append((i, 1, row[i]))
    return sum(row), start, runs


NC, ROW0, RUNS = staircase(TOPK)
NC8, ROW0_8, RUNS8 = staircase(8)
PAIRS = [i * TOPK + j for i in range(TOPK) for j in range(TOPK // (i + 1))]

NSIM = 2 * HEADS * KEYS
SIMW = NSIM + NC
SCH = 3
CW = SIMW // SCH
TAKEN = -2.0 ** 126

C_TOK, C_ATT, C_ID, C_CEN, C_DOWN = 0, 512, 1024, 1152, 1280
C_COL = C_DOWN + NC
C_END = C_COL + 7
COL_B, COL_BQ, COL_BK, COL_BV, COL_BO, COL_ME, COL_MO = range(7)


def wait(eng, sem, value):
    if not (isinstance(value, int) and value <= 0):
        eng.wait_ge(sem, value)


def build(nc, x, wpack, qkpack, up, out):
    out_rows = out.rearrange("b p d -> (b p) d")

    with ExitStack() as ctx:
        def sb(name, shape):
            return ctx.enter_context(nc.sbuf_tensor(name, shape, F32))

        def bank(name):
            return ctx.enter_context(nc.psum_tensor(name, [128, 512], F32))

        def sem(name):
            return ctx.enter_context(nc.semaphore(name))

        w_tok = sb("w_tok", [128, NCH, DM])
        w_att = sb("w_att", [128, 4, DM])
        ident = sb("ident", [128, 128])
        center = sb("center", [128, 128])
        cols = sb("cols", [128, 7])
        w_sim = sb("w_sim", [128, SIMW])
        qk = sb("qk", [64, 2 * HEADS * (DM + KEYS)])
        w_up = sb("w_up", [128, DM])
        bq_even = sb("bq_even", [128, 1])
        bq_odd = sb("bq_odd", [128, 1])
        bo_all = sb("bo_all", [128, 1])
        xT = sb("xT", [128, GB, 2, NSEG])
        hT = [sb(f"hT{i}", [128, COLS]) for i in range(2)]
        hR = sb("hR", [128, COLS])
        hc = sb("hc", [NP, GB, DM])
        ss = sb("ss", [NP, GB])
        var = sb("var", [NP, GB])
        rstd = sb("rstd", [NP, GB])
        junk = sb("junk", [128, 2, GB, DM])
        power = sb("power", [128, GB])
        xn = sb("xn", [NP, GB, DM])
        xnT = sb("xnT", [128, COLS])
        q_even = [sb(f"q_even{i}", [128, COLS]) for i in range(2)]
        q_odd = [sb(f"q_odd{i}", [128, COLS]) for i in range(2)]
        kT = [sb(f"kT{i}", [128, COLS]) for i in range(2)]
        vx = [sb(f"vx{i}", [NP, GB, HEADS, 32]) for i in range(2)]
        negm = sb("negm", [NP, 8, 4])
        probs = [sb(f"probs{i}", [NP, 4, NP]) for i in range(2)]
        probsT = [sb(f"probsT{i}", [NP, 4, NP]) for i in range(2)]
        cu = sb("cu", [128, 2, COLS])
        rl = sb("rl", [NP, 16])
        ctx_tok = sb("ctx_tok", [NP, GB, DM])
        ctxT = sb("ctxT", [128, COLS])
        h2T = [sb(f"h2T{i}", [128, COLS]) for i in range(2)]
        hc2 = sb("hc2", [128, TILES, DM])
        ss2 = sb("ss2", [128, TILES])
        var2 = sb("var2", [128, TILES])
        rstd2 = sb("rstd2", [128, TILES])
        xn2 = sb("xn2", [128, TILES, DM])
        xn2T = sb("xn2T", [128, TILES, 128])
        h2R = sb("h2R", [128, COLS])
        sims = sb("sims", [128, TILES, SIMW])
        best = sb("best", [128, TILES, 2, HEADS, TOPK])
        cand = sb("cand", [128, TILES, HEADS, NC])
        cand8 = sb("cand8", [128, TILES, HEADS, NC8])
        left = sb("left", [128, TILES, HEADS, NC])
        top = sb("top", [128, TILES, HEADS, TOPK])
        shifted = sb("shifted", [128, TILES, HEADS * (NC + TOPK)])
        expd = sb("expd", [128, TILES, HEADS * (NC + TOPK)])
        taken = sb("taken", [128, TILES, HEADS, NC])
        den = sb("den", [128, TILES, HEADS])
        rden = sb("rden", [128, TILES, HEADS])
        wsel = sb("wsel", [128, HEADS, NC])
        wnorm = sb("wnorm", [128, HEADS, NC])
        wsum4 = sb("wsum4", [128, 4, NC])
        wsum2 = sb("wsum2", [128, 2, NC])
        wsum1 = sb("wsum1", [128, NC])
        gel = sb("gel", [128, TILES, NC])
        u = sb("u", [128, TILES, 128])
        uT = sb("uT", [128, TILES, 128])
        out_sb = sb("out_sb", [128, TILES, DM])

        W0, W1, S0, S1, PT, CT, F0, F1 = [bank(f"ps{i}") for i in range(8)]
        S = [S0, S1]
        FB = [F0, F1]

        dve_passed, pool_passed = sem("dve_passed"), sem("pool_passed")
        first_loaded = sem("first_loaded")
        ffn_loaded = sem("ffn_loaded")
        filled = sem("filled")
        wsim_ps = sem("wsim_ps")
        wsim_ready = sem("wsim_ready")
        bo_ps = sem("bo_ps")
        x_loaded = sem("x_loaded")
        tok_ps = sem("tok_ps")
        hT_ready = sem("hT_ready")
        hc_ps = sem("hc_ps")
        hc_ready = sem("hc_ready")
        ln1 = sem("ln1")
        xn_ready = sem("xn_ready")
        xnT_ps = sem("xnT_ps")
        xnT_ready = sem("xnT_ready")
        q_ps, k_ps, v_ps = sem("q_ps"), sem("k_ps"), sem("v_ps")
        q_ready, k_ready, v_ready = sem("q_ready"), sem("k_ready"), sem("v_ready")
        hR_ready = sem("hR_ready")
        s_ps = sem("s_ps")
        max_ready = sem("max_ready")
        exp_ready = sem("exp_ready")
        pT_ps = sem("pT_ps")
        pT_ready = sem("pT_ready")
        pv_ps = sem("pv_ps")
        cu_ready = sem("cu_ready")
        cuT_ps = sem("cuT_ps")
        rl_ready = sem("rl_ready")
        ctx_ready = sem("ctx_ready")
        ctxT_ps, ctxT_ready = sem("ctxT_ps"), sem("ctxT_ready")
        h2_ps, h2T_ready = sem("h2_ps"), sem("h2T_ready")
        hc2_ps, hc2_ready = sem("hc2_ps"), sem("hc2_ready")
        ln2 = sem("ln2")
        xn2_ready = sem("xn2_ready")
        xn2T_ps, xn2T_ready = sem("xn2T_ps"), sem("xn2T_ready")
        sim_ps, sim_ready = sem("sim_ps"), sem("sim_ready")
        best_done = sem("best_done")
        cand_ready = sem("cand_ready")
        top_done = sem("top_done")
        gel_ready = sem("gel_ready")
        h2R_ready = sem("h2R_ready")
        shifted_ready = sem("shifted_ready")
        weights_exp = sem("weights_exp")
        den_ready, rden_ready = sem("den_ready"), sem("rden_ready")
        wchain = sem("wchain")
        u_ready = sem("u_ready")
        uT_ps, uT_ready = sem("uT_ps"), sem("uT_ready")
        out_ps, out_ready = sem("out_ps"), sem("out_ready")
        stored = [sem(f"stored{t}") for t in range(TILES)]

        N_FIRST, N_FFN = 16 * 5, 16 * 3

        FIRST, LAST = 6, NG - 2

        def steps(step):
            for g in range(-1, FIRST):
                step(g, g)
            with step.engine.Fori(FIRST, LAST - 1, 2) as g:
                step(g, FIRST)
                step(g + 1, FIRST + 1)
            for g in range(LAST, NG + 4):
                step(g, g)

        def has(group):
            return 0 <= group < NG

        def own_wait(eng, passed):
            eng.sem_inc(passed, 1)

        block = ctx.enter_context(nc.Block())

        @block.sync
        def _(sp):
            sp.dma_start(w_tok[:], wpack[:, C_TOK:C_ATT].rearrange("p (c d) -> p c d", c=NCH)).then_inc(first_loaded, 16)
            sp.dma_start(xT[:], x[0]).then_inc(x_loaded, 16)
            sp.dma_start(cols[:], wpack[:, C_COL:C_END]).then_inc(first_loaded, 16)
            sp.dma_start(center[:], wpack[:, C_CEN:C_DOWN]).then_inc(first_loaded, 16)
            sp.dma_start(ident[:], wpack[:, C_ID:C_CEN]).then_inc(first_loaded, 16)
            sp.dma_start(w_att[:], wpack[:, C_ATT:C_ID].rearrange("p (c d) -> p c d", c=4)).then_inc(first_loaded, 16)
            sp.dma_start(w_sim[:, NSIM:SIMW], wpack[:, C_DOWN:C_COL]).then_inc(ffn_loaded, 16)
            sp.dma_start(qk[:], qkpack).then_inc(ffn_loaded, 16)
            sp.wait_ge(filled, 1)
            sp.dma_start(w_up[0:NC, :], up).then_inc(ffn_loaded, 16)

            def step(g, G):
                if has(G + 2):
                    sp.wait_ge(tok_ps, g + 2)
                    sp.dma_start(xT[:], x[g + 2]).then_inc(x_loaded, 16)
                if has(G - 3):
                    e = g - 3
                    sp.wait_ge(out_ready, e + 1)
                    for t in range(TILES):
                        row = COLS * e + T0[t] + SKIP[t]
                        sp.dma_start(out_rows[bass.ds(row, 128 - SKIP[t]), :],
                                     out_sb[SKIP[t]:128, t, :]).then_inc(stored[t], 16)

            step.engine = sp
            steps(step)
            for t in range(TILES):
                sp.wait_ge(stored[t], 16 * NG)

        @block.tensor
        def _(pe):
            mm, tr = nc.tensor.matmul, nc.tensor.transpose

            def front_tok(g):
                pe.wait_ge(x_loaded, 16 * (g + 1))
                wait(pe, v_ready, g)
                wait(pe, out_ready, g - 4)
                for c in range(NCH):
                    last = mm(W0[:, 0:COLS], w_tok[:, c, :], xT[:, :, c % 2, c // 2:c // 2 + NP],
                              start=(c == 0), stop=(c == NCH - 1))
                last.then_inc(tok_ps, 1)

            def front_center(g, G):
                pe.wait_ge(hT_ready, g + 1)
                for b in range(GB):
                    last = mm(W0[0:NP, b * DM:(b + 1) * DM], hT[G % 2][:, b * NP:(b + 1) * NP], center[:],
                              start=True, stop=True)
                last.then_inc(hc_ps, 1)

            def front_xnT(g):
                pe.wait_ge(xn_ready, g + 1)
                for b in range(GB):
                    last = tr(W0[:, b * NP:(b + 1) * NP], xn[:, b, :], ident[0:NP, 0:NP])
                last.then_inc(xnT_ps, 1)

            def front_q(g):
                pe.wait_ge(xnT_ready, g + 1)
                mm(W0[:, 0:COLS], w_att[:, 0, :], xnT[:], start=True, stop=True).then_inc(q_ps, 1)

            def front_k(g):
                wait(pe, hc2_ready, g - 1)
                mm(W1[:, 0:COLS], w_att[:, 1, :], xnT[:], start=True, stop=True).then_inc(k_ps, 1)

            def front_v(g):
                pe.wait_ge(q_ready, g + 1)
                for b in range(GB):
                    last = mm(W0[0:NP, b * DM:(b + 1) * DM], xnT[:, b * NP:(b + 1) * NP],
                              w_att[:, 2, :], start=True, stop=True)
                last.then_inc(v_ps, 1)

            def scores(g, G, n):
                pair, strip = n // 4, n % 4
                if n == 0:
                    pe.wait_ge(q_ready, g + 1)
                    pe.wait_ge(k_ready, g + 1)
                wait(pe, exp_ready, 8 * g + n - 1)
                r = 32 * strip
                for j in range(4):
                    b, q = 2 * pair + j // 2, (q_even, q_odd)[j % 2][G % 2]
                    last = mm(S[n % 2][0:NP, j * NP:(j + 1) * NP], q[r:r + 32, b * NP:(b + 1) * NP],
                              kT[G % 2][r:r + 32, b * NP:(b + 1) * NP], start=True, stop=True)
                last.then_inc(s_ps, 1)

            def probs_T(g, n):
                pe.wait_ge(exp_ready, 8 * g + n + 1)
                wait(pe, pT_ready, 8 * g + n)
                for j in range(4):
                    last = tr(PT[0:NP, j * NP:(j + 1) * NP], probs[n % 2][:, j, :], ident[0:NP, 0:NP])
                last.then_inc(pT_ps, 1)

            def values(g, G, n):
                pair, strip = n // 4, n % 4
                pe.wait_ge(pT_ready, 8 * g + n + 1)
                if n == 0:
                    pe.wait_ge(v_ready, g + 1)
                if n % 4 == 0:
                    wait(pe, cu_ready, 2 * g + n // 4)
                for j in range(4):
                    b, h = j // 2, 2 * strip + j % 2
                    at = (2 * b + h // 4) * NP
                    last = mm(CT[32 * (h % 4):32 * (h % 4) + 32, at:at + NP],
                              vx[G % 2][:, 2 * pair + b, h, :], probsT[n % 2][:, j, :], start=True, stop=True)
                last.then_inc(pv_ps, 1)

            def ctx_back(g, pair):
                pe.wait_ge(cu_ready, 2 * g + pair + 1)
                if pair == 0:
                    wait(pe, xn2T_ready, g)
                else:
                    pe.wait_ge(ctx_ready, 2 * g + 1)
                for i in range(4):
                    last = tr(W1[0:NP, i * 128:(i + 1) * 128], cu[:, pair, i * NP:(i + 1) * NP], ident[:])
                last.then_inc(cuT_ps, 1)

            def tail_ctxT(g):
                pe.wait_ge(ctx_ready, 2 * g + 2)
                for b in range(GB):
                    last = tr(W1[:, b * NP:(b + 1) * NP], ctx_tok[:, b, :], ident[0:NP, 0:NP])
                last.then_inc(ctxT_ps, 1)

            def tail_h2(g):
                pe.wait_ge(ctxT_ready, g + 1)
                pe.wait_ge(hR_ready, g + 1)
                mm(W1[:, 0:COLS], w_att[:, 3, :], ctxT[:], start=True, stop=False)
                mm(W1[:, 0:COLS], ident[:], hR[:], start=False, stop=True).then_inc(h2_ps, 1)

            def tail_center(g, G):
                pe.wait_ge(h2T_ready, g + 1)
                for t in range(TILES):
                    last = mm(W1[:, t * 128:(t + 1) * 128], h2T[G % 2][:, T0[t]:T0[t] + 128], center[:],
                              start=True, stop=True)
                last.then_inc(hc2_ps, 1)

            def tail_xn2T(g, G):
                pe.wait_ge(xn2_ready, g + 1)
                if has(G + 2):
                    pe.wait_ge(k_ready, g + 3)
                for t in range(TILES):
                    last = tr(W1[:, t * 128:(t + 1) * 128], xn2[:, t, :], ident[:])
                last.then_inc(xn2T_ps, 1)

            def sim(f, fG, t, k):
                c = SCH * t + k
                if c == 0:
                    pe.wait_ge(xn2T_ready, f + 1)
                    if fG == 0:
                        pe.wait_ge(wsim_ready, 3)
                wait(pe, sim_ready, 9 * f + c - 1)
                mm(FB[(fG + c) % 2][:, 0:CW], xn2T[:, t, :], w_sim[:, k * CW:(k + 1) * CW],
                   start=True, stop=True).then_inc(sim_ps, 1)

            def late_uT(e, G):
                pe.wait_ge(u_ready, TILES * e + TILES)
                if has(G + 4):
                    pe.wait_ge(v_ready, e + 5)
                wait(pe, out_ready, e)
                for t in range(TILES):
                    last = tr(W0[:, t * 128:(t + 1) * 128], u[:, t, :], ident[:])
                last.then_inc(uT_ps, 1)

            def late_out(e):
                pe.wait_ge(uT_ready, e + 1)
                pe.wait_ge(h2R_ready, e + 1)
                for t in range(TILES):
                    at = W0[:, t * DM:(t + 1) * DM]
                    mm(at, uT[:, t, :], w_up[:], start=True, stop=False)
                    last = mm(at, h2R[:, T0[t]:T0[t] + 128], ident[:], start=False, stop=True)
                last.then_inc(out_ps, 1)

            def fold_keys():
                pe.wait_ge(ffn_loaded, N_FFN)
                for i in range(2 * HEADS):
                    last = mm(FB[i // HEADS][:, (i % HEADS) * KEYS:(i % HEADS + 1) * KEYS],
                              qk[:, i * DM:(i + 1) * DM],
                              qk[:, 2 * HEADS * DM + i * KEYS:2 * HEADS * DM + (i + 1) * KEYS],
                              start=True, stop=True)
                    if i % HEADS == HEADS - 1:
                        last.then_inc(wsim_ps, 1)

            pe.wait_ge(first_loaded, N_FIRST)
            mm(CT[:, 0:1], w_att[:, 3, :], cols[:, COL_BV:COL_BV + 1], start=True, stop=True).then_inc(bo_ps, 1)
            pe.wait_ge(filled, 5)

            def step(g, G):
                slot = [[] for _ in range(8)]
                if has(G + 1):
                    slot[0].append(lambda: front_tok(g + 1))
                if has(G - 2):
                    for i, (t, k) in zip((0, 0, 1, 2, 3, 4), [(t, k) for t in (1, 2) for k in range(SCH)]):
                        slot[i].append(lambda t=t, k=k: sim(g - 2, G - 2, t, k))
                if has(G - 1):
                    slot[0].append(lambda: ctx_back(g - 1, 1))
                    slot[1].append(lambda: tail_ctxT(g - 1))
                    slot[2].append(lambda: tail_h2(g - 1))
                    slot[3].append(lambda: tail_center(g - 1, G - 1))
                if has(G + 1):
                    slot[1].append(lambda: front_center(g + 1, G + 1))
                    slot[3].append(lambda: front_xnT(g + 1))
                    slot[4].append(lambda: front_q(g + 1))
                    slot[4].append(lambda: front_k(g + 1))
                    slot[5].append(lambda: front_v(g + 1))
                if has(G):
                    slot[6].append(lambda: ctx_back(g, 0))
                if has(G - 1):
                    slot[5].append(lambda: tail_xn2T(g - 1, G - 1))
                    for i, k in zip((6, 6, 7), range(SCH)):
                        slot[i].append(lambda k=k: sim(g - 1, G - 1, 0, k))
                if has(G - 3):
                    slot[6].append(lambda: late_uT(g - 3, G - 3))
                    slot[7].append(lambda: late_out(g - 3))
                for n in range(8):
                    if n < 6 and has(G):
                        scores(g, G, n + 2)
                    if n >= 6 and has(G + 1):
                        scores(g + 1, G + 1, n - 6)
                    if has(G):
                        probs_T(g, n)
                    if n >= 1 and has(G):
                        values(g, G, n - 1)
                    if n == 0 and has(G - 1):
                        values(g - 1, G - 1, 7)
                    for part in slot[n]:
                        part()
                    if n == 2 and G == -1:
                        fold_keys()

            step.engine = pe
            steps(step)

        @block.scalar
        def _(act):
            run = nc.scalar.activation

            def bias(i):
                return cols[:, i:i + 1]

            def front_hT(g, G):
                act.wait_ge(tok_ps, g + 1)
                wait(act, hR_ready, g - 1)
                run(hT[G % 2][:], W0[:, 0:COLS], ACT.Identity, bias=bias(COL_B)).then_inc(hT_ready, 1)

            def front_hc(g):
                act.wait_ge(hc_ps, g + 1)
                run(hc[:], W0[0:NP, :].rearrange("p (b d) -> p b d", b=GB), ACT.Copy)
                for b in range(GB):
                    last = run(junk[0:NP, 0, b, :], W0[0:NP, b * DM:(b + 1) * DM], ACT.Square,
                               accum_out=ss[:, b:b + 1])
                last.then_inc(hc_ready, 1)

            def save_h(g, G):
                act.wait_ge(hT_ready, g + 1)
                wait(act, h2_ps, g)
                run(hR[:], hT[G % 2][:], ACT.Copy).then_inc(hR_ready, 1)

            def save_h2(e, G):
                act.wait_ge(h2T_ready, e + 1)
                wait(act, out_ps, e)
                run(h2R[:], h2T[G % 2][:], ACT.Copy).then_inc(h2R_ready, 1)

            def front_xnT(g):
                act.wait_ge(xnT_ps, g + 1)
                run(xnT[:], W0[:, 0:COLS], ACT.Copy).then_inc(xnT_ready, 1)

            def front_q(g, G):
                act.wait_ge(q_ps, g + 1)
                run(q_even[G % 2][:], W0[:, 0:COLS], ACT.Identity, bias=bq_even[:], scale=bias(COL_ME))
                run(q_odd[G % 2][:], W0[:, 0:COLS], ACT.Identity, bias=bq_odd[:], scale=bias(COL_MO)).then_inc(q_ready, 1)

            def front_k(g, G):
                act.wait_ge(k_ps, g + 1)
                run(kT[G % 2][:], W1[:, 0:COLS], ACT.Identity, bias=bias(COL_BK)).then_inc(k_ready, 1)

            def front_v(g, G):
                act.wait_ge(v_ps, g + 1)
                run(vx[G % 2][:, :, :, 0:DK], W0[0:NP, :].rearrange("p (b h d) -> p b h d", b=GB, h=HEADS),
                    ACT.Copy).then_inc(v_ready, 1)

            def exps(g, n):
                act.wait_ge(max_ready, 8 * g + n + 1)
                wait(act, pT_ps, 8 * g + n - 1)
                for j in range(4):
                    last = run(probs[n % 2][:, j, :], S[n % 2][0:NP, j * NP:(j + 1) * NP], ACT.Exp,
                               bias=negm[:, n, j:j + 1])
                last.then_inc(exp_ready, 1)

            def copy_pT(g, n):
                act.wait_ge(pT_ps, 8 * g + n + 1)
                wait(act, pv_ps, 8 * g + n - 1)
                run(probsT[n % 2][:], PT[0:NP, 0:COLS].rearrange("p (j q) -> p j q", j=4),
                    ACT.Copy).then_inc(pT_ready, 1)

            def copy_cu(g, pair):
                act.wait_ge(pv_ps, 8 * g + 4 * pair + 4)
                run(cu[:, pair, :], CT[:, 0:COLS], ACT.Copy).then_inc(cu_ready, 1)

            def tail_ctxT(g):
                act.wait_ge(ctxT_ps, g + 1)
                run(ctxT[:], W1[:, 0:COLS], ACT.Copy).then_inc(ctxT_ready, 1)

            def tail_h2(g, G):
                act.wait_ge(h2_ps, g + 1)
                wait(act, h2R_ready, g - 1)
                run(h2T[G % 2][:], W1[:, 0:COLS], ACT.Identity, bias=bo_all[:]).then_inc(h2T_ready, 1)

            def tail_hc(g):
                act.wait_ge(hc2_ps, g + 1)
                run(hc2[:], W1[:, 0:TILES * DM].rearrange("p (t d) -> p t d", t=TILES), ACT.Copy)
                for t in range(TILES):
                    last = run(junk[:, 1, t, :], W1[:, t * DM:(t + 1) * DM], ACT.Square, accum_out=ss2[:, t:t + 1])
                last.then_inc(hc2_ready, 1)

            def tail_xn2T(g):
                act.wait_ge(xn2T_ps, g + 1)
                run(xn2T[:], W1[:, 0:TILES * 128].rearrange("p (t d) -> p t d", t=TILES),
                    ACT.Copy).then_inc(xn2T_ready, 1)

            def copy_sim(f, fG, t, k):
                c = SCH * t + k
                act.wait_ge(sim_ps, 9 * f + c + 1)
                if k == 0:
                    wait(act, best_done, 18 * (f - 1) + 6 * t + 6)
                if c == 2:
                    wait(act, gel_ready, f)
                run(sims[:, t, k * CW:(k + 1) * CW], FB[(fG + c) % 2][:, 0:CW], ACT.Copy).then_inc(sim_ready, 1)

            def gelu(f):
                act.wait_ge(sim_ready, 9 * f + 9)
                wait(act, u_ready, TILES * f)
                run(gel[:], sims[:, :, NSIM:SIMW], ACT.Gelu).then_inc(gel_ready, 1)

            def late_exp(e, t):
                act.wait_ge(shifted_ready, TILES * e + t + 1)
                wait(act, u_ready, TILES * e)
                run(expd[:, t, :], shifted[:, t, :], ACT.Exp)
                run(taken[:, t, :, :], left[:, t, :, :], ACT.Relu, scale=1.0 / TAKEN,
                    ).then_inc(weights_exp, 1)

            def late_uT(e):
                act.wait_ge(uT_ps, e + 1)
                run(uT[:], W0[:, 0:TILES * 128].rearrange("p (t d) -> p t d", t=TILES),
                    ACT.Copy).then_inc(uT_ready, 1)

            def late_out(e):
                act.wait_ge(out_ps, e + 1)
                for t in range(TILES):
                    wait(act, stored[t], 16 * e)
                run(out_sb[:], W0[:, 0:TILES * DM].rearrange("p (t d) -> p t d", t=TILES),
                    ACT.Copy).then_inc(out_ready, 1)

            def copy_wsim():
                for i in range(2):
                    act.wait_ge(wsim_ps, i + 1)
                    run(w_sim[:, i * 512:(i + 1) * 512], FB[i][:], ACT.Copy).then_inc(wsim_ready, 1)

            act.wait_ge(bo_ps, 1)
            run(bo_all[:], CT[:, 0:1], ACT.Identity, bias=bias(COL_BO)).then_inc(wsim_ready, 1)
            act.wait_ge(filled, 5)

            def step(g, G):
                slot = [[] for _ in range(8)]

                def put(i, part, *args):
                    slot[i].append(lambda: part(*args))

                if has(G - 4):
                    put(0, late_out, g - 4)
                if has(G - 2):
                    put(0, copy_sim, g - 2, G - 2, 0, 2)
                if has(G - 3):
                    put(0, save_h2, g - 3, G - 3)
                    put(0, late_exp, g - 3, 0)
                if has(G - 1):
                    put(0, copy_cu, g - 1, 1)
                if has(G + 1):
                    put(1, front_hT, g + 1, G + 1)
                if has(G - 2):
                    put(1, copy_sim, g - 2, G - 2, 1, 0)
                    put(1, copy_sim, g - 2, G - 2, 1, 1)
                if has(G - 3):
                    put(1, late_exp, g - 3, 1)
                if has(G - 1):
                    put(2, tail_ctxT, g - 1)
                if has(G + 1):
                    put(2, front_hc, g + 1)
                if has(G - 2):
                    put(2, copy_sim, g - 2, G - 2, 1, 2)
                if has(G - 1):
                    put(3, tail_h2, g - 1, G - 1)
                if has(G - 2):
                    put(3, copy_sim, g - 2, G - 2, 2, 0)
                if has(G - 3):
                    put(3, late_exp, g - 3, 2)
                if has(G):
                    put(3, save_h, g, G)
                if has(G + 1):
                    put(4, front_xnT, g + 1)
                if has(G - 1):
                    put(4, tail_hc, g - 1)
                if has(G - 2):
                    put(4, copy_sim, g - 2, G - 2, 2, 1)
                if has(G + 1):
                    put(5, front_q, g + 1, G + 1)
                    put(5, front_k, g + 1, G + 1)
                if has(G):
                    put(5, copy_cu, g, 0)
                if has(G - 2):
                    put(5, copy_sim, g - 2, G - 2, 2, 2)
                if has(G + 1):
                    put(6, front_v, g + 1, G + 1)
                if has(G - 1):
                    put(6, tail_xn2T, g - 1)
                if has(G - 3):
                    put(7, late_uT, g - 3)
                if has(G - 1):
                    put(7, copy_sim, g - 1, G - 1, 0, 0)
                    put(7, copy_sim, g - 1, G - 1, 0, 1)
                if has(G - 2):
                    put(7, gelu, g - 2)
                for n in range(8):
                    if has(G):
                        exps(g, n)
                    if n >= 1 and has(G):
                        copy_pT(g, n - 1)
                    if n == 0 and has(G - 1):
                        copy_pT(g - 1, 7)
                    for part in slot[n]:
                        part()
                    if n == 5 and G == -1:
                        copy_wsim()

            step.engine = act
            steps(step)

        @block.vector
        def _(dve):
            def first_topk(f, t, i):
                p, rnd = i % 2, i // 2
                base = 18 * f + 6 * t
                if i == 0:
                    dve.wait_ge(sim_ready, 9 * f + SCH * t + 3)
                    wait(dve, cand_ready, TILES * (f - 1) + t + 1)
                if rnd:
                    dve.wait_ge(best_done, base + i - 1)
                own_wait(dve, dve_passed)
                for h in range(HEADS):
                    at = (p * HEADS + h) * KEYS
                    src = sims[:, t, at:at + KEYS]
                    if rnd == 0:
                        last = dve.max(best[:, t, p, h, 0:8], src)
                    elif rnd == 1:
                        last = dve.match_replace(out=src, in_to_replace=best[:, t, p, h, 0:8],
                                                 in_values=src, imm_value=TAKEN)
                    else:
                        last = dve.max(best[:, t, p, h, 8:16], src)
                last.then_inc(best_done, 1)

            def second_topk(f, t, i):
                rnd = i // 2
                base = 24 * f + 8 * t
                if i == 0:
                    dve.wait_ge(cand_ready, TILES * f + t + 1)
                    wait(dve, shifted_ready, TILES * (f - 1) + t + 1)
                    wait(dve, weights_exp, TILES * (f - 1) + t + 1)
                if rnd:
                    dve.wait_ge(top_done, base + i - 1)
                own_wait(dve, dve_passed)
                for h in range(4 * (i % 2), 4 * (i % 2) + 4):
                    if rnd == 0:
                        last = dve.max(top[:, t, h, 0:8], cand8[:, t, h, :])
                    elif rnd == 1:
                        last = dve.match_replace(out=left[:, t, h, :], in_to_replace=top[:, t, h, 0:8],
                                                 in_values=cand[:, t, h, :], imm_value=TAKEN)
                    elif rnd == 2:
                        last = dve.max(top[:, t, h, 8:16], left[:, t, h, :])
                    else:
                        last = dve.match_replace(out=left[:, t, h, :], in_to_replace=top[:, t, h, 8:16],
                                                 in_values=left[:, t, h, :], imm_value=TAKEN)
                last.then_inc(top_done, 1)

            def row_max(g, n):
                dve.wait_ge(s_ps, 8 * g + n + 1)
                dve.tensor_reduce(negm[:, n, :], S[n % 2][0:NP, 0:COLS].rearrange("p (j k) -> p j k", j=4),
                                  AX_X, ALU.max, negate=True).then_inc(max_ready, 1)

            def normalise(g, pair):
                dve.wait_ge(cuT_ps, 2 * g + pair + 1)
                src = W1[0:NP, :].rearrange("p (i c) -> p i c", c=32)
                dve.reciprocal(rl[:], src[:, :, DK]).then_inc(rl_ready, 1)
                dve.wait_ge(rl_ready, 2 * g + pair + 1)
                dst = ctx_tok[:, 2 * pair:2 * pair + 2, :].rearrange("p b (h d) -> p (b h) d", d=DK)
                dve.tensor_tensor(dst, src[:, :, 0:DK], rl[:].unsqueeze(2).to_broadcast([NP, 16, DK]),
                                  ALU.mult).then_inc(ctx_ready, 1)

            def denominator(e, t):
                dve.wait_ge(weights_exp, TILES * e + t + 1)
                wait(dve, u_ready, TILES * e)
                dve.tensor_reduce(den[:, t, :], expd[:, t, HEADS * NC:].rearrange("p (h k) -> p h k", h=HEADS),
                                  AX_X, ALU.add).then_inc(den_ready, 1)
                dve.wait_ge(den_ready, TILES * e + t + 1)
                dve.reciprocal(rden[:, t, :], den[:, t, :]).then_inc(rden_ready, 1)

            dve.memset(w_up[:], 0.0).then_inc(filled, 1)
            for v in vx:
                last = dve.memset(v[:], 0.0)
            last.then_inc(filled, 1)
            dve.memset(u[:], 0.0)
            dve.memset(power[:], -0.5).then_inc(filled, 1)
            dve.wait_ge(filled, 3)
            for v in vx:
                last = dve.memset(v[:, :, :, DK:DK + 1], 1.0)
            last.then_inc(filled, 1)
            dve.wait_ge(first_loaded, N_FIRST)
            dve.tensor_tensor(bq_even[:], cols[:, COL_BQ:COL_BQ + 1], cols[:, COL_ME:COL_ME + 1], ALU.mult)
            dve.tensor_tensor(bq_odd[:], cols[:, COL_BQ:COL_BQ + 1], cols[:, COL_MO:COL_MO + 1],
                              ALU.mult).then_inc(filled, 1)

            def step(g, G):
                f, e = g - 2, g - 3
                work = []
                for what, has_it, group, t, k in (
                        (second_topk, has(G - 3), e, 2, 8), (first_topk, has(G - 2), f, 0, 6),
                        (first_topk, has(G - 2), f, 1, 6), (second_topk, has(G - 2), f, 0, 8),
                        (first_topk, has(G - 2), f, 2, 6), (second_topk, has(G - 2), f, 1, 8)):
                    for i in range(k):
                        work.append([lambda what=what, group=group, t=t, i=i: what(group, t, i)] if has_it else [])

                def put(i, part, *args):
                    work[i].append(lambda: part(*args))

                for i, n in zip((3, 9, 12, 16, 19, 26), range(2, 8)):
                    if has(G):
                        put(i, row_max, g, n)
                for i, n in zip((30, 35), range(2)):
                    if has(G + 1):
                        put(i, row_max, g + 1, n)
                if has(G - 3):
                    for t, i in enumerate((5, 10, 17)):
                        put(i, denominator, e, t)
                if has(G - 1):
                    put(8, normalise, g - 1, 1)
                if has(G):
                    put(32, normalise, g, 0)
                for parts in work:
                    for part in parts:
                        part()

            step.engine = dve
            steps(step)

        @block.gpsimd
        def _(pool):
            tt, ts = nc.gpsimd.tensor_tensor, nc.gpsimd.tensor_scalar

            def layernorm(ready, chain, done, g, squares, v, r, src, dst, n):
                pool.wait_ge(ready, g + 1)
                own_wait(pool, pool_passed)
                ts(v[:], squares[:], 1.0 / DM, EPS, ALU.mult, ALU.add).then_inc(chain, 1)
                pool.wait_ge(chain, 2 * g + 1)
                tt(r[:], v[:], power[0:v.shape[0], 0:n], ALU.pow).then_inc(chain, 1)
                pool.wait_ge(chain, 2 * g + 2)
                tt(dst[:], src[:], r[:].unsqueeze(2).to_broadcast([v.shape[0], n, DM]), ALU.mult).then_inc(done, 1)

            def front_ln(g):
                layernorm(hc_ready, ln1, xn_ready, g, ss, var, rstd, hc, xn, GB)

            def tail_ln(g):
                layernorm(hc2_ready, ln2, xn2_ready, g, ss2, var2, rstd2, hc2, xn2, TILES)

            def sums(f, t):
                pool.wait_ge(best_done, 18 * f + 6 * t + 6)
                wait(pool, top_done, 24 * (f - 1) + 8 * t + 8)
                for sums_of, starts, runs in ((cand8, ROW0_8, RUNS8), (cand, ROW0, RUNS)):
                    for i, n, w in runs:
                        dst = sums_of[:, t, :, starts[i]:starts[i] + n * w].rearrange("p h (n w) -> p h n w", n=n)
                        sx = best[:, t, 0, :, i:i + n].unsqueeze(3).to_broadcast([128, HEADS, n, w])
                        sy = best[:, t, 1, :, 0:w].unsqueeze(2).to_broadcast([128, HEADS, n, w])
                        last = tt(dst, sx, sy, ALU.add)
                last.then_inc(cand_ready, 1)

            def shift(e, t):
                pool.wait_ge(top_done, 24 * e + 8 * t + 8)
                wait(pool, weights_exp, TILES * e)
                tt(shifted[:, t, 0:HEADS * NC].rearrange("p (h c) -> p h c", h=HEADS), cand[:, t, :, :],
                   top[:, t, :, 0:1].to_broadcast([128, HEADS, NC]), ALU.subtract)
                tt(shifted[:, t, HEADS * NC:].rearrange("p (h c) -> p h c", h=HEADS), top[:, t, :, :],
                   top[:, t, :, 0:1].to_broadcast([128, HEADS, TOPK]), ALU.subtract).then_inc(shifted_ready, 1)

            def weigh(e, t):
                base = 5 * (TILES * e + t)
                pool.wait_ge(weights_exp, TILES * e + t + 1)
                tt(wsel[:], expd[:, t, 0:HEADS * NC].rearrange("p (h c) -> p h c", h=HEADS),
                   taken[:, t, :, :], ALU.mult).then_inc(wchain, 1)
                pool.wait_ge(wchain, base + 1)
                pool.wait_ge(rden_ready, TILES * e + t + 1)
                tt(wnorm[:], wsel[:], rden[:, t, :].unsqueeze(2).to_broadcast([128, HEADS, NC]),
                   ALU.mult).then_inc(wchain, 1)
                pool.wait_ge(wchain, base + 2)
                tt(wsum4[:], wnorm[:, 0:4, :], wnorm[:, 4:8, :], ALU.add).then_inc(wchain, 1)
                pool.wait_ge(wchain, base + 3)
                tt(wsum2[:], wsum4[:, 0:2, :], wsum4[:, 2:4, :], ALU.add).then_inc(wchain, 1)
                pool.wait_ge(wchain, base + 4)
                tt(wsum1[:], wsum2[:, 0, :], wsum2[:, 1, :], ALU.add).then_inc(wchain, 1)
                pool.wait_ge(wchain, base + 5)
                pool.wait_ge(gel_ready, e + 1)
                wait(pool, uT_ps, e)
                tt(u[:, t, 0:NC], wsum1[:], gel[:, t, :], ALU.mult).then_inc(u_ready, 1)

            pool.wait_ge(filled, 5)

            def step(g, G):
                f, e = g - 2, g - 3
                if has(G - 3):
                    shift(e, 0)
                    shift(e, 1)
                    weigh(e, 0)
                    shift(e, 2)
                if has(G + 1):
                    front_ln(g + 1)
                if has(G - 2):
                    sums(f, 0)
                if has(G - 3):
                    weigh(e, 1)
                if has(G - 1):
                    tail_ln(g - 1)
                if has(G - 2):
                    sums(f, 1)
                if has(G - 3):
                    weigh(e, 2)
                if has(G - 2):
                    sums(f, 2)

            step.engine = pool
            steps(step)


def kernel(x, L0_tok_W, L0_tok_b, L0_attn_Wq, L0_attn_bq, L0_attn_Wk, L0_attn_bk, L0_attn_Wv, L0_attn_bv,
           L0_attn_Wo, L0_attn_bo, L0_ffn_W_q, L0_ffn_keys, L0_ffn_down_embed, L0_ffn_up_embed):
    import numpy as np
    import concourse.bacc as bacc
    from concourse.bass_utils import run_bass_kernel_spmd

    segs = np.asarray(x)[:, :NSEG * STRIDE, :].reshape(NG, GB, NSEG, 2, 128)
    x_dev = np.ascontiguousarray(segs.transpose(0, 4, 1, 3, 2))

    tokW = np.asarray(L0_tok_W).T.reshape(NCH, 128, DM).transpose(1, 0, 2).reshape(128, NCH * DM)
    row = np.arange(128)
    even = (row // DK % 2 == 0).astype(np.float32) * DK ** -0.5
    odd = (row // DK % 2 == 1).astype(np.float32) * DK ** -0.5
    ident = np.eye(128, dtype=np.float32)
    center = (np.eye(DM) - 1.0 / DM).astype(np.float32)
    down = np.asarray(L0_ffn_down_embed)[PAIRS].T
    columns = [np.asarray(v)[:, None] for v in (L0_tok_b, L0_attn_bq, L0_attn_bk, L0_attn_bv, L0_attn_bo, even, odd)]
    wpack = np.ascontiguousarray(np.concatenate(
        [tokW, np.asarray(L0_attn_Wq), np.asarray(L0_attn_Wk), np.asarray(L0_attn_Wv), np.asarray(L0_attn_Wo),
         ident, center, down, *columns], axis=1))

    wq = np.asarray(L0_ffn_W_q).reshape(DM, 2 * HEADS, DKEY).transpose(2, 1, 0).reshape(DKEY, -1)
    keys = np.asarray(L0_ffn_keys).transpose(3, 2, 0, 1).reshape(DKEY, -1)
    qkpack = np.ascontiguousarray(np.concatenate([wq, keys], axis=1))
    up = np.ascontiguousarray(np.asarray(L0_ffn_up_embed)[PAIRS])

    nc = bacc.Bacc("TRN2", target_bir_lowering=False, num_devices=1)
    arrays = {"x_dram": x_dev, "wpack_dram": wpack, "qkpack_dram": qkpack, "up_dram": up}
    args = [nc.dram_tensor(name, a.shape, F32, kind="ExternalInput").ap() for name, a in arrays.items()]
    out = nc.dram_tensor("out_0_dram", (BATCH, NP, DM), F32, kind="ExternalOutput").ap()
    build(nc, *args, out)
    r = run_bass_kernel_spmd(nc, [arrays], core_ids=[0])
    return r.results[0]["out_0_dram"]
```

```python
from contextlib import ExitStack

import concourse.bass as bass
from concourse import mybir

F32 = mybir.dt.float32
ALU = mybir.AluOpType
ACT = mybir.ActivationFunctionType
AX_X = mybir.AxisListType.X

BATCH, SEQ, FEAT = 64, 750, 32
PATCH, STRIDE = 16, 8
DM = 128
NP = (SEQ - PATCH) // STRIDE + 1
NSEG = NP + 1
NCH = PATCH * FEAT // 128
HEADS, DK = 8, 16
KEYS, DKEY, TOPK = 64, 64, 16
EPS = 1e-5

GB = 4
NG = BATCH // GB
COLS = GB * NP
TILES = 3
T0 = [0, 128, COLS - 128]
SKIP = [0, 0, 2 * 128 - (COLS - 128)]

def staircase(k):
    row = [k // (i + 1) for i in range(k)]
    start = [sum(row[:i]) for i in range(k)]
    runs = []
    for i in range(k):
        if runs and runs[-1][2] == row[i]:
            runs[-1] = (runs[-1][0], runs[-1][1] + 1, row[i])
        else:
            runs.append((i, 1, row[i]))
    return sum(row), start, runs


NC, ROW0, RUNS = staircase(TOPK)
NC8, ROW0_8, RUNS8 = staircase(8)
NROW8 = ROW0[8]
PAIRS = [i * TOPK + j for i in range(TOPK) for j in range(TOPK // (i + 1))]

NSIM = 2 * HEADS * KEYS
SIMW = NSIM + NC
SCH = 3
CW = SIMW // SCH
TAKEN = -2.0 ** 126

C_TOK, C_ATT, C_ID, C_CEN, C_DOWN = 0, 512, 1024, 1152, 1280
C_COL = C_DOWN + NC
C_END = C_COL + 7
COL_B, COL_BQ, COL_BK, COL_BV, COL_BO, COL_ME, COL_MO = range(7)


def wait(eng, sem, value):
    if not (isinstance(value, int) and value <= 0):
        eng.wait_ge(sem, value)


def build(nc, x, wpack, qkpack, up, out):
    out_rows = out.rearrange("b p d -> (b p) d")

    with ExitStack() as ctx:
        def sb(name, shape):
            return ctx.enter_context(nc.sbuf_tensor(name, shape, F32))

        def bank(name):
            return ctx.enter_context(nc.psum_tensor(name, [128, 512], F32))

        def sem(name):
            return ctx.enter_context(nc.semaphore(name))

        w_tok = sb("w_tok", [128, NCH, DM])
        w_att = sb("w_att", [128, 4, DM])
        ident = sb("ident", [128, 128])
        center = sb("center", [128, 128])
        cols = sb("cols", [128, 7])
        w_sim = sb("w_sim", [128, SIMW])
        qk = sb("qk", [64, 2 * HEADS * (DM + KEYS)])
        w_up = sb("w_up", [128, DM])
        bq_even = sb("bq_even", [128, 1])
        bq_odd = sb("bq_odd", [128, 1])
        bo_all = sb("bo_all", [128, 1])
        xT = sb("xT", [128, GB, 2, NSEG])
        hT = [sb(f"hT{i}", [128, COLS]) for i in range(2)]
        hR = sb("hR", [128, COLS])
        hc = sb("hc", [NP, GB, DM])
        ss = sb("ss", [NP, GB])
        var = sb("var", [NP, GB])
        rstd = sb("rstd", [NP, GB])
        junk = sb("junk", [128, 2, GB, DM])
        power = sb("power", [128, GB])
        xn = sb("xn", [NP, GB, DM])
        xnT = sb("xnT", [128, COLS])
        q_even = [sb(f"q_even{i}", [128, COLS]) for i in range(2)]
        q_odd = [sb(f"q_odd{i}", [128, COLS]) for i in range(2)]
        kT = [sb(f"kT{i}", [128, COLS]) for i in range(2)]
        vx = [sb(f"vx{i}", [NP, GB, HEADS, 32]) for i in range(2)]
        negm = sb("negm", [NP, 8, 4])
        probs = [sb(f"probs{i}", [NP, 4, NP]) for i in range(2)]
        probsT = [sb(f"probsT{i}", [NP, 4, NP]) for i in range(2)]
        cu = sb("cu", [128, 2, COLS])
        ctx_raw = sb("ctx_raw", [NP, 16, 32])
        rl = sb("rl", [NP, 16])
        ctx_tok = sb("ctx_tok", [NP, GB, DM])
        ctxT = sb("ctxT", [128, COLS])
        h2T = [sb(f"h2T{i}", [128, COLS]) for i in range(2)]
        hc2 = sb("hc2", [128, TILES, DM])
        ss2 = sb("ss2", [128, TILES])
        var2 = sb("var2", [128, TILES])
        rstd2 = sb("rstd2", [128, TILES])
        xn2 = sb("xn2", [128, TILES, DM])
        xn2T = sb("xn2T", [128, TILES, 128])
        h2R = sb("h2R", [128, COLS])
        sims = sb("sims", [128, TILES, SIMW])
        best = sb("best", [128, TILES, 2, HEADS, TOPK])
        cand = sb("cand", [128, TILES, HEADS, NC])
        cand8 = sb("cand8", [128, TILES, HEADS, NC8])
        left = sb("left", [128, TILES, HEADS, NC])
        top = sb("top", [128, TILES, HEADS, TOPK])
        shifted = sb("shifted", [128, TILES, HEADS * (NC + TOPK)])
        expd = sb("expd", [128, TILES, HEADS * (NC + TOPK)])
        taken = sb("taken", [128, TILES, HEADS, NC])
        den = sb("den", [128, TILES, HEADS])
        rden = sb("rden", [128, TILES, HEADS])
        den8 = sb("den8", [128, TILES, HEADS, 8])
        den4 = sb("den4", [128, TILES, HEADS, 4])
        den2 = sb("den2", [128, TILES, HEADS, 2])
        wsel = sb("wsel", [128, TILES, HEADS, NC])
        wnorm = sb("wnorm", [128, TILES, HEADS, NC])
        wsum4 = sb("wsum4", [128, TILES, 4, NC])
        wsum2 = sb("wsum2", [128, TILES, 2, NC])
        wsum1 = sb("wsum1", [128, TILES, NC])
        gel = sb("gel", [128, TILES, NC])
        u = sb("u", [128, TILES, 128])
        uT = sb("uT", [128, TILES, 128])
        out_sb = sb("out_sb", [128, TILES, DM])

        W0, W1, S0, S1, PT, CT, F0, F1 = [bank(f"ps{i}") for i in range(8)]
        S = [S0, S1]
        FB = [F0, F1]

        dve_passed, pool_passed = sem("dve_passed"), sem("pool_passed")
        first_loaded = sem("first_loaded")
        ffn_loaded = sem("ffn_loaded")
        filled = sem("filled")
        wsim_ps = sem("wsim_ps")
        wsim_ready = sem("wsim_ready")
        bo_ps = sem("bo_ps")
        x_loaded = sem("x_loaded")
        tok_ps = sem("tok_ps")
        hT_ready = sem("hT_ready")
        hc_ps = sem("hc_ps")
        hc_ready = sem("hc_ready")
        ln1 = sem("ln1")
        xn_ready = sem("xn_ready")
        xnT_ps = sem("xnT_ps")
        xnT_ready = sem("xnT_ready")
        q_ps, k_ps, v_ps = sem("q_ps"), sem("k_ps"), sem("v_ps")
        q_ready, k_ready, v_ready = sem("q_ready"), sem("k_ready"), sem("v_ready")
        hR_ready = sem("hR_ready")
        s_ps = sem("s_ps")
        max_ready = sem("max_ready")
        exp_ready = sem("exp_ready")
        pT_ps = sem("pT_ps")
        pT_ready = sem("pT_ready")
        pv_ps = sem("pv_ps")
        cu_ready = sem("cu_ready")
        cuT_ps = sem("cuT_ps")
        ctx_copied = sem("ctx_copied")
        rl_ready = sem("rl_ready")
        ctx_ready = sem("ctx_ready")
        ctxT_ps, ctxT_ready = sem("ctxT_ps"), sem("ctxT_ready")
        h2_ps, h2T_ready = sem("h2_ps"), sem("h2T_ready")
        hc2_ps, hc2_ready = sem("hc2_ps"), sem("hc2_ready")
        ln2 = sem("ln2")
        xn2_ready = sem("xn2_ready")
        xn2T_ps, xn2T_ready = sem("xn2T_ps"), sem("xn2T_ready")
        sim_ps, sim_ready = sem("sim_ps"), sem("sim_ready")
        best_done = sem("best_done")
        cand_ready = sem("cand_ready")
        top_done = sem("top_done")
        gel_ready = sem("gel_ready")
        h2R_ready = sem("h2R_ready")
        shifted_ready = sem("shifted_ready")
        weights_exp = sem("weights_exp")
        den_ready, rden_ready = sem("den_ready"), sem("rden_ready")
        den_chain, wchain = sem("den_chain"), sem("wchain")
        last_shifted, last_chain, last_u = sem("last_shifted"), sem("last_chain"), sem("last_u")
        u_ready = sem("u_ready")
        uT_ps, uT_ready = sem("uT_ps"), sem("uT_ready")
        out_ps, out_ready = sem("out_ps"), sem("out_ready")
        stored = [sem(f"stored{t}") for t in range(TILES)]

        N_FIRST, N_FFN = 16 * 5, 16 * 3

        FIRST, LAST = 6, NG - 2

        def steps(step):
            for g in range(-1, FIRST):
                step(g, g)
            with step.engine.Fori(FIRST, LAST - 1, 2) as g:
                step(g, FIRST)
                step(g + 1, FIRST + 1)
            for g in range(LAST, NG + 4):
                step(g, g)

        def has(group):
            return 0 <= group < NG

        def late_parts(group):
            return [(t, range(t, t + 1)) for t in range(TILES)] if group == NG - 1 else [(0, range(TILES))]

        def own_wait(eng, passed):
            eng.sem_inc(passed, 1)

        block = ctx.enter_context(nc.Block())

        @block.sync
        def _(sp):
            sp.dma_start(w_tok[:],
                         wpack[:, C_TOK:C_ATT].rearrange("p (c d) -> p c d", c=NCH)).then_inc(first_loaded, 16)
            sp.dma_start(xT[:], x[0]).then_inc(x_loaded, 16)
            sp.dma_start(cols[:], wpack[:, C_COL:C_END]).then_inc(first_loaded, 16)
            sp.dma_start(center[:], wpack[:, C_CEN:C_DOWN]).then_inc(first_loaded, 16)
            sp.dma_start(ident[:], wpack[:, C_ID:C_CEN]).then_inc(first_loaded, 16)
            sp.dma_start(w_att[:], wpack[:, C_ATT:C_ID].rearrange("p (c d) -> p c d", c=4)).then_inc(first_loaded, 16)
            sp.dma_start(w_sim[:, NSIM:SIMW], wpack[:, C_DOWN:C_COL]).then_inc(ffn_loaded, 16)
            sp.dma_start(qk[:], qkpack).then_inc(ffn_loaded, 16)
            sp.wait_ge(filled, 1)
            sp.dma_start(w_up[0:NC, :], up).then_inc(ffn_loaded, 16)

            def step(g, G):
                if has(G + 2):
                    sp.wait_ge(tok_ps, g + 2)
                    sp.dma_start(xT[:], x[g + 2]).then_inc(x_loaded, 16)
                if has(G - 3):
                    for n, tiles in late_parts(G - 3):
                        sp.wait_ge(out_ready, g - 3 + n + 1)
                        for t in tiles:
                            row = COLS * (g - 3) + T0[t] + SKIP[t]
                            sp.dma_start(out_rows[bass.ds(row, 128 - SKIP[t]), :],
                                         out_sb[SKIP[t]:128, t, :]).then_inc(stored[t], 16)

            step.engine = sp
            steps(step)
            for t in range(TILES):
                sp.wait_ge(stored[t], 16 * NG)

        @block.tensor
        def _(pe):
            mm, tr = nc.tensor.matmul, nc.tensor.transpose

            def front_tok(g):
                pe.wait_ge(x_loaded, 16 * (g + 1))
                wait(pe, v_ready, g)
                wait(pe, out_ready, g - 4)
                for c in range(NCH):
                    last = mm(W0[:, 0:COLS], w_tok[:, c, :], xT[:, :, c % 2, c // 2:c // 2 + NP],
                              start=(c == 0), stop=(c == NCH - 1))
                last.then_inc(tok_ps, 1)

            def front_center(g, G):
                pe.wait_ge(hT_ready, g + 1)
                for b in range(GB):
                    last = mm(W0[0:NP, b * DM:(b + 1) * DM], hT[G % 2][:, b * NP:(b + 1) * NP], center[:],
                              start=True, stop=True)
                last.then_inc(hc_ps, 1)

            def front_xnT(g):
                pe.wait_ge(xn_ready, g + 1)
                for b in range(GB):
                    last = tr(W0[:, b * NP:(b + 1) * NP], xn[:, b, :], ident[0:NP, 0:NP])
                last.then_inc(xnT_ps, 1)

            def front_q(g):
                pe.wait_ge(xnT_ready, g + 1)
                mm(W0[:, 0:COLS], w_att[:, 0, :], xnT[:], start=True, stop=True).then_inc(q_ps, 1)

            def front_k(g):
                wait(pe, hc2_ready, g - 1)
                mm(W1[:, 0:COLS], w_att[:, 1, :], xnT[:], start=True, stop=True).then_inc(k_ps, 1)

            def front_v(g):
                pe.wait_ge(q_ready, g + 1)
                for b in range(GB):
                    last = mm(W0[0:NP, b * DM:(b + 1) * DM], xnT[:, b * NP:(b + 1) * NP],
                              w_att[:, 2, :], start=True, stop=True)
                last.then_inc(v_ps, 1)

            def scores(g, G, n):
                pair, strip = n // 4, n % 4
                if n == 0:
                    pe.wait_ge(q_ready, g + 1)
                    pe.wait_ge(k_ready, g + 1)
                wait(pe, exp_ready, 8 * g + n - 1)
                r = 32 * strip
                for j in range(4):
                    b, q = 2 * pair + j // 2, (q_even, q_odd)[j % 2][G % 2]
                    last = mm(S[n % 2][0:NP, j * NP:(j + 1) * NP], q[r:r + 32, b * NP:(b + 1) * NP],
                              kT[G % 2][r:r + 32, b * NP:(b + 1) * NP], start=True, stop=True)
                last.then_inc(s_ps, 1)

            def probs_T(g, n):
                pe.wait_ge(exp_ready, 8 * g + n + 1)
                wait(pe, pT_ready, 8 * g + n)
                for j in range(4):
                    last = tr(PT[0:NP, j * NP:(j + 1) * NP], probs[n % 2][:, j, :], ident[0:NP, 0:NP])
                last.then_inc(pT_ps, 1)

            def values(g, G, n):
                pair, strip = n // 4, n % 4
                pe.wait_ge(pT_ready, 8 * g + n + 1)
                if n == 0:
                    pe.wait_ge(v_ready, g + 1)
                if n % 4 == 0:
                    wait(pe, cu_ready, 2 * g + n // 4)
                for j in range(4):
                    b, h = j // 2, 2 * strip + j % 2
                    at = (2 * b + h // 4) * NP
                    last = mm(CT[32 * (h % 4):32 * (h % 4) + 32, at:at + NP],
                              vx[G % 2][:, 2 * pair + b, h, :], probsT[n % 2][:, j, :], start=True, stop=True)
                last.then_inc(pv_ps, 1)

            def ctx_back(g, pair):
                pe.wait_ge(cu_ready, 2 * g + pair + 1)
                if pair == 0:
                    wait(pe, xn2T_ready, g)
                else:
                    pe.wait_ge(ctx_copied, 2 * g + 1)
                for i in range(4):
                    last = tr(W1[0:NP, i * 128:(i + 1) * 128], cu[:, pair, i * NP:(i + 1) * NP], ident[:])
                last.then_inc(cuT_ps, 1)

            def tail_ctxT(g):
                pe.wait_ge(ctx_ready, 2 * g + 2)
                for b in range(GB):
                    last = tr(W1[:, b * NP:(b + 1) * NP], ctx_tok[:, b, :], ident[0:NP, 0:NP])
                last.then_inc(ctxT_ps, 1)

            def tail_h2(g):
                pe.wait_ge(ctxT_ready, g + 1)
                pe.wait_ge(hR_ready, g + 1)
                mm(W1[:, 0:COLS], w_att[:, 3, :], ctxT[:], start=True, stop=False)
                mm(W1[:, 0:COLS], ident[:], hR[:], start=False, stop=True).then_inc(h2_ps, 1)

            def tail_center(g, G):
                pe.wait_ge(h2T_ready, g + 1)
                for t in range(TILES):
                    last = mm(W1[:, t * 128:(t + 1) * 128], h2T[G % 2][:, T0[t]:T0[t] + 128], center[:],
                              start=True, stop=True)
                last.then_inc(hc2_ps, 1)

            def tail_xn2T(g, G):
                pe.wait_ge(xn2_ready, g + 1)
                if has(G + 2):
                    pe.wait_ge(k_ready, g + 3)
                for t in range(TILES):
                    last = tr(W1[:, t * 128:(t + 1) * 128], xn2[:, t, :], ident[:])
                last.then_inc(xn2T_ps, 1)

            def sim(f, fG, t, k):
                c = SCH * t + k
                if c == 0:
                    pe.wait_ge(xn2T_ready, f + 1)
                    if fG == 0:
                        pe.wait_ge(wsim_ready, 3)
                wait(pe, sim_ready, 9 * f + c - 1)
                mm(FB[(fG + c) % 2][:, 0:CW], xn2T[:, t, :], w_sim[:, k * CW:(k + 1) * CW],
                   start=True, stop=True).then_inc(sim_ps, 1)

            def late_uT(e, G, n, tiles):
                if n == TILES - 1:
                    pe.wait_ge(last_u, 1)
                else:
                    pe.wait_ge(u_ready, e + n + 1)
                if has(G + 4):
                    pe.wait_ge(v_ready, e + 5)
                wait(pe, out_ready, e + n)
                for t in tiles:
                    last = tr(W0[:, t * 128:(t + 1) * 128], u[:, t, :], ident[:])
                last.then_inc(uT_ps, 1)

            def late_out(e, n, tiles):
                pe.wait_ge(uT_ready, e + n + 1)
                pe.wait_ge(h2R_ready, e + 1)
                for t in tiles:
                    at = W0[:, t * DM:(t + 1) * DM]
                    mm(at, uT[:, t, :], w_up[:], start=True, stop=False)
                    last = mm(at, h2R[:, T0[t]:T0[t] + 128], ident[:], start=False, stop=True)
                last.then_inc(out_ps, 1)

            def fold_keys():
                pe.wait_ge(ffn_loaded, N_FFN)
                for i in range(2 * HEADS):
                    last = mm(FB[i // HEADS][:, (i % HEADS) * KEYS:(i % HEADS + 1) * KEYS],
                              qk[:, i * DM:(i + 1) * DM],
                              qk[:, 2 * HEADS * DM + i * KEYS:2 * HEADS * DM + (i + 1) * KEYS],
                              start=True, stop=True)
                    if i % HEADS == HEADS - 1:
                        last.then_inc(wsim_ps, 1)

            pe.wait_ge(first_loaded, N_FIRST)
            mm(CT[:, 0:1], w_att[:, 3, :], cols[:, COL_BV:COL_BV + 1], start=True, stop=True).then_inc(bo_ps, 1)
            pe.wait_ge(filled, 5)

            def step(g, G):
                slot = [[] for _ in range(8)]

                def put(i, part, *args):
                    slot[i].append(lambda: part(*args))

                if has(G - 1):
                    put(0, ctx_back, g - 1, 1)
                if has(G + 1):
                    put(0, front_tok, g + 1)
                if has(G - 2):
                    for i, (t, k) in zip((0, 0, 2, 2, 3, 4), [(t, k) for t in (1, 2) for k in range(SCH)]):
                        put(i, sim, g - 2, G - 2, t, k)
                if has(G - 1):
                    put(1, tail_ctxT, g - 1)
                    put(2, tail_h2, g - 1)
                    put(3, tail_center, g - 1, G - 1)
                if has(G + 1):
                    put(1, front_center, g + 1, G + 1)
                    put(3, front_xnT, g + 1)
                    put(4, front_q, g + 1)
                    put(4, front_k, g + 1)
                    put(5, front_v, g + 1)
                if has(G):
                    put(6, ctx_back, g, 0)
                if has(G - 1):
                    put(5, tail_xn2T, g - 1, G - 1)
                    for i, k in zip((6, 6, 7), range(SCH)):
                        put(i, sim, g - 1, G - 1, 0, k)
                if has(G - 3):
                    for n, tiles in late_parts(G - 3):
                        put(6 + min(n, 1), late_uT, g - 3, G - 3, n, tiles)
                        put(7, late_out, g - 3, n, tiles)
                for n in range(8):
                    if n < 6 and has(G):
                        scores(g, G, n + 2)
                    if n >= 6 and has(G + 1):
                        scores(g + 1, G + 1, n - 6)
                    if has(G):
                        probs_T(g, n)
                    if n >= 1 and has(G):
                        values(g, G, n - 1)
                    if n == 0 and has(G - 1):
                        values(g - 1, G - 1, 7)
                    for part in slot[n]:
                        part()
                    if n == 2 and G == -1:
                        fold_keys()

            step.engine = pe
            steps(step)

        @block.scalar
        def _(act):
            run = nc.scalar.activation

            def bias(i):
                return cols[:, i:i + 1]

            def front_hT(g, G):
                act.wait_ge(tok_ps, g + 1)
                wait(act, hR_ready, g - 1)
                run(hT[G % 2][:], W0[:, 0:COLS], ACT.Identity, bias=bias(COL_B)).then_inc(hT_ready, 1)

            def front_hc(g):
                act.wait_ge(hc_ps, g + 1)
                run(hc[:], W0[0:NP, :].rearrange("p (b d) -> p b d", b=GB), ACT.Copy)
                for b in range(GB):
                    last = run(junk[0:NP, 0, b, :], W0[0:NP, b * DM:(b + 1) * DM], ACT.Square,
                               accum_out=ss[:, b:b + 1])
                last.then_inc(hc_ready, 1)

            def save_h(g, G):
                act.wait_ge(hT_ready, g + 1)
                wait(act, h2_ps, g)
                run(hR[:], hT[G % 2][:], ACT.Copy).then_inc(hR_ready, 1)

            def save_h2(e, G):
                act.wait_ge(h2T_ready, e + 1)
                wait(act, out_ps, e)
                run(h2R[:], h2T[G % 2][:], ACT.Copy).then_inc(h2R_ready, 1)

            def front_xnT(g):
                act.wait_ge(xnT_ps, g + 1)
                run(xnT[:], W0[:, 0:COLS], ACT.Copy).then_inc(xnT_ready, 1)

            def front_q(g, G):
                act.wait_ge(q_ps, g + 1)
                run(q_even[G % 2][:], W0[:, 0:COLS], ACT.Identity, bias=bq_even[:], scale=bias(COL_ME))
                run(q_odd[G % 2][:], W0[:, 0:COLS], ACT.Identity, bias=bq_odd[:],
                    scale=bias(COL_MO)).then_inc(q_ready, 1)

            def front_k(g, G):
                act.wait_ge(k_ps, g + 1)
                run(kT[G % 2][:], W1[:, 0:COLS], ACT.Identity, bias=bias(COL_BK)).then_inc(k_ready, 1)

            def front_v(g, G):
                act.wait_ge(v_ps, g + 1)
                run(vx[G % 2][:, :, :, 0:DK], W0[0:NP, :].rearrange("p (b h d) -> p b h d", b=GB, h=HEADS),
                    ACT.Copy).then_inc(v_ready, 1)

            def exps(g, n):
                act.wait_ge(max_ready, 8 * g + n + 1)
                wait(act, pT_ps, 8 * g + n - 1)
                for j in range(4):
                    last = run(probs[n % 2][:, j, :], S[n % 2][0:NP, j * NP:(j + 1) * NP], ACT.Exp,
                               bias=negm[:, n, j:j + 1])
                last.then_inc(exp_ready, 1)

            def copy_pT(g, n):
                act.wait_ge(pT_ps, 8 * g + n + 1)
                wait(act, pv_ps, 8 * g + n - 1)
                run(probsT[n % 2][:], PT[0:NP, 0:COLS].rearrange("p (j q) -> p j q", j=4),
                    ACT.Copy).then_inc(pT_ready, 1)

            def copy_cu(g, pair):
                act.wait_ge(pv_ps, 8 * g + 4 * pair + 4)
                run(cu[:, pair, :], CT[:, 0:COLS], ACT.Copy).then_inc(cu_ready, 1)

            def copy_ctx(g, pair):
                act.wait_ge(cuT_ps, 2 * g + pair + 1)
                wait(act, ctx_ready, 2 * g + pair)
                run(ctx_raw[:], W1[0:NP, :].rearrange("p (i c) -> p i c", c=32), ACT.Copy).then_inc(ctx_copied, 1)

            def tail_ctxT(g):
                act.wait_ge(ctxT_ps, g + 1)
                run(ctxT[:], W1[:, 0:COLS], ACT.Copy).then_inc(ctxT_ready, 1)

            def tail_h2(g, G):
                act.wait_ge(h2_ps, g + 1)
                wait(act, h2R_ready, g - 1)
                run(h2T[G % 2][:], W1[:, 0:COLS], ACT.Identity, bias=bo_all[:]).then_inc(h2T_ready, 1)

            def tail_hc(g):
                act.wait_ge(hc2_ps, g + 1)
                run(hc2[:], W1[:, 0:TILES * DM].rearrange("p (t d) -> p t d", t=TILES), ACT.Copy)
                for t in range(TILES):
                    last = run(junk[:, 1, t, :], W1[:, t * DM:(t + 1) * DM], ACT.Square, accum_out=ss2[:, t:t + 1])
                last.then_inc(hc2_ready, 1)

            def tail_xn2T(g):
                act.wait_ge(xn2T_ps, g + 1)
                run(xn2T[:], W1[:, 0:TILES * 128].rearrange("p (t d) -> p t d", t=TILES),
                    ACT.Copy).then_inc(xn2T_ready, 1)

            def copy_sim(f, fG, t, k):
                c = SCH * t + k
                act.wait_ge(sim_ps, 9 * f + c + 1)
                if k == 0:
                    wait(act, best_done, 18 * (f - 1) + 6 * t + 6)
                if c == 2:
                    wait(act, gel_ready, f)
                run(sims[:, t, k * CW:(k + 1) * CW], FB[(fG + c) % 2][:, 0:CW], ACT.Copy).then_inc(sim_ready, 1)

            def gelu(f):
                act.wait_ge(sim_ready, 9 * f + 9)
                wait(act, u_ready, f)
                run(gel[:], sims[:, :, NSIM:SIMW], ACT.Gelu).then_inc(gel_ready, 1)

            def late_exp(e, t, last=False):
                if last:
                    act.wait_ge(last_shifted, 1)
                else:
                    act.wait_ge(shifted_ready, TILES * e + t + 1)
                wait(act, u_ready, e)
                run(expd[:, t, :], shifted[:, t, :], ACT.Exp)
                run(taken[:, t, :, :], left[:, t, :, :], ACT.Relu, scale=1.0 / TAKEN).then_inc(weights_exp, 1)

            def late_uT(e, n, tiles):
                act.wait_ge(uT_ps, e + n + 1)
                run(uT[:, tiles[0]:tiles[-1] + 1, :],
                    W0[:, tiles[0] * 128:(tiles[-1] + 1) * 128].rearrange("p (t d) -> p t d", d=128),
                    ACT.Copy).then_inc(uT_ready, 1)

            def late_out(e, n, tiles):
                act.wait_ge(out_ps, e + n + 1)
                for t in tiles:
                    wait(act, stored[t], 16 * e)
                run(out_sb[:, tiles[0]:tiles[-1] + 1, :],
                    W0[:, tiles[0] * DM:(tiles[-1] + 1) * DM].rearrange("p (t d) -> p t d", d=DM),
                    ACT.Copy).then_inc(out_ready, 1)

            def copy_wsim():
                for i in range(2):
                    act.wait_ge(wsim_ps, i + 1)
                    run(w_sim[:, i * 512:(i + 1) * 512], FB[i][:], ACT.Copy).then_inc(wsim_ready, 1)

            act.wait_ge(bo_ps, 1)
            run(bo_all[:], CT[:, 0:1], ACT.Identity, bias=bias(COL_BO)).then_inc(wsim_ready, 1)
            act.wait_ge(filled, 5)

            def step(g, G):
                slot = [[] for _ in range(8)]

                def put(i, part, *args):
                    slot[i].append(lambda: part(*args))

                if has(G - 1):
                    put(0, copy_cu, g - 1, 1)
                if has(G - 4) and G - 4 < NG - 1:
                    put(0, late_out, g - 4, 0, range(TILES))
                if has(G - 2):
                    put(0, copy_sim, g - 2, G - 2, 0, 2)
                if has(G - 3):
                    put(1, save_h2, g - 3, G - 3)
                    if G - 3 < NG - 1:
                        put(1, late_exp, g - 3, 0)
                if has(G - 1):
                    put(0, copy_ctx, g - 1, 1)
                if has(G + 1):
                    put(1, front_hT, g + 1, G + 1)
                if has(G - 2):
                    put(1, copy_sim, g - 2, G - 2, 1, 0)
                    put(2, copy_sim, g - 2, G - 2, 1, 1)
                if has(G - 3) and G - 3 < NG - 1:
                    put(2, late_exp, g - 3, 1)
                if has(G - 1):
                    put(2, tail_ctxT, g - 1)
                if has(G + 1):
                    put(2, front_hc, g + 1)
                if has(G - 2):
                    put(2, copy_sim, g - 2, G - 2, 1, 2)
                if has(G - 1):
                    put(3, tail_h2, g - 1, G - 1)
                if has(G - 2):
                    put(4, copy_sim, g - 2, G - 2, 2, 0)
                if has(G - 3) and G - 3 < NG - 1:
                    put(3, late_exp, g - 3, 2)
                if has(G):
                    put(4, save_h, g, G)
                if has(G + 1):
                    put(4, front_xnT, g + 1)
                if has(G - 1):
                    put(3, tail_hc, g - 1)
                if has(G - 2):
                    put(4, copy_sim, g - 2, G - 2, 2, 1)
                if has(G + 1):
                    put(5, front_q, g + 1, G + 1)
                    put(5, front_k, g + 1, G + 1)
                if has(G):
                    put(4, copy_cu, g, 0)
                if has(G - 2):
                    put(5, copy_sim, g - 2, G - 2, 2, 2)
                if has(G + 1):
                    put(6, front_v, g + 1, G + 1)
                if has(G - 1):
                    put(6, tail_xn2T, g - 1)
                if G - 2 == NG - 1:
                    put(7, late_exp, g - 2, 0)
                if G - 3 == NG - 1:
                    put(7, late_exp, g - 3, 1)
                    put(7, late_exp, g - 3, 2, True)
                    for n, tiles in late_parts(G - 3):
                        put(7, late_uT, g - 3, n, tiles)
                        put(7, late_out, g - 3, n, tiles)
                elif has(G - 3):
                    put(7, late_uT, g - 3, 0, range(TILES))
                if has(G):
                    put(7, copy_ctx, g, 0)
                if has(G - 1):
                    put(6, copy_sim, g - 1, G - 1, 0, 0)
                    put(7, copy_sim, g - 1, G - 1, 0, 1)
                if has(G - 2):
                    put(7, gelu, g - 2)
                for n in range(8):
                    if has(G):
                        exps(g, n)
                    if n >= 1 and has(G):
                        copy_pT(g, n - 1)
                    if n == 0 and has(G - 1):
                        copy_pT(g - 1, 7)
                    for part in slot[n]:
                        part()
                    if n == 5 and G == -1:
                        copy_wsim()

            step.engine = act
            steps(step)

        @block.vector
        def _(dve):
            def first_topk(f, t, i):
                p, rnd = i % 2, i // 2
                base = 18 * f + 6 * t
                if i == 0:
                    dve.wait_ge(sim_ready, 9 * f + SCH * t + 3)
                    wait(dve, cand_ready, TILES * (f - 1) + t + 1)
                if rnd:
                    dve.wait_ge(best_done, base + i - 1)
                own_wait(dve, dve_passed)
                for h in range(HEADS):
                    at = (p * HEADS + h) * KEYS
                    src = sims[:, t, at:at + KEYS]
                    if rnd == 0:
                        last = dve.max(best[:, t, p, h, 0:8], src)
                    elif rnd == 1:
                        last = dve.match_replace(out=src, in_to_replace=best[:, t, p, h, 0:8],
                                                 in_values=src, imm_value=TAKEN)
                    else:
                        last = dve.max(best[:, t, p, h, 8:16], src)
                last.then_inc(best_done, 1)

            def second_topk(f, t, i):
                rnd = i // 2
                base = 24 * f + 8 * t
                if i == 0:
                    dve.wait_ge(cand_ready, TILES * f + t + 1)
                    wait(dve, shifted_ready, TILES * (f - 1) + t + 1)
                    wait(dve, weights_exp, TILES * (f - 1) + t + 1)
                if rnd:
                    dve.wait_ge(top_done, base + i - 1)
                own_wait(dve, dve_passed)
                for h in range(4 * (i % 2), 4 * (i % 2) + 4):
                    if rnd == 0:
                        last = dve.max(top[:, t, h, 0:8], cand8[:, t, h, :])
                    elif rnd == 1:
                        last = dve.match_replace(out=left[:, t, h, 0:NROW8], in_to_replace=top[:, t, h, 0:8],
                                                 in_values=cand[:, t, h, 0:NROW8], imm_value=TAKEN)
                    elif rnd == 2:
                        last = dve.max(top[:, t, h, 8:16], left[:, t, h, 1:])
                    else:
                        last = dve.match_replace(out=left[:, t, h, 1:], in_to_replace=top[:, t, h, 8:16],
                                                 in_values=left[:, t, h, 1:], imm_value=TAKEN)
                last.then_inc(top_done, 1)

            def row_max(g, n):
                dve.wait_ge(s_ps, 8 * g + n + 1)
                dve.tensor_reduce(negm[:, n, :], S[n % 2][0:NP, 0:COLS].rearrange("p (j k) -> p j k", j=4),
                                  AX_X, ALU.max, negate=True).then_inc(max_ready, 1)

            def invert_sums(g, pair):
                dve.wait_ge(ctx_copied, 2 * g + pair + 1)
                wait(dve, ctx_ready, 2 * g + pair)
                dve.reciprocal(rl[:], ctx_raw[:, :, DK]).then_inc(rl_ready, 1)

            def last_shift(e, t):
                dve.wait_ge(top_done, 24 * e + 8 * t + 8)
                dve.wait_ge(weights_exp, TILES * e)
                nc.vector.tensor_tensor(shifted[:, t, 0:HEADS * NC].rearrange("p (h c) -> p h c", h=HEADS),
                                        cand[:, t, :, :], top[:, t, :, 0:1].to_broadcast([128, HEADS, NC]),
                                        ALU.subtract)
                nc.vector.tensor_tensor(shifted[:, t, HEADS * NC:].rearrange("p (h c) -> p h c", h=HEADS),
                                        top[:, t, :, :], top[:, t, :, 0:1].to_broadcast([128, HEADS, TOPK]),
                                        ALU.subtract).then_inc(last_shifted, 1)

            def last_weigh(e, t):
                tt = nc.vector.tensor_tensor
                dve.wait_ge(weights_exp, TILES * e + t + 1)
                dve.tensor_reduce(den[:, t, :], expd[:, t, HEADS * NC:].rearrange("p (h k) -> p h k", h=HEADS),
                                  AX_X, ALU.add).then_inc(last_chain, 1)
                tt(wsel[:, t], expd[:, t, 0:HEADS * NC].rearrange("p (h c) -> p h c", h=HEADS),
                   taken[:, t], ALU.mult).then_inc(last_chain, 1)
                dve.wait_ge(last_chain, 1)
                dve.reciprocal(rden[:, t, :], den[:, t, :]).then_inc(last_chain, 1)
                dve.wait_ge(last_chain, 3)
                tt(wnorm[:, t], wsel[:, t], rden[:, t, :].unsqueeze(2).to_broadcast([128, HEADS, NC]),
                   ALU.mult).then_inc(last_chain, 1)
                dve.wait_ge(last_chain, 4)
                tt(wsum4[:, t], wnorm[:, t, 0:4], wnorm[:, t, 4:8], ALU.add).then_inc(last_chain, 1)
                dve.wait_ge(last_chain, 5)
                tt(wsum2[:, t], wsum4[:, t, 0:2], wsum4[:, t, 2:4], ALU.add).then_inc(last_chain, 1)
                dve.wait_ge(last_chain, 6)
                tt(wsum1[:, t], wsum2[:, t, 0], wsum2[:, t, 1], ALU.add).then_inc(last_chain, 1)
                dve.wait_ge(last_chain, 7)
                dve.wait_ge(gel_ready, e + 1)
                dve.wait_ge(uT_ps, e)
                tt(u[:, t, 0:NC], wsum1[:, t], gel[:, t], ALU.mult).then_inc(last_u, 1)

            def invert_den(e, n, tiles):
                dve.wait_ge(den_ready, e + n + 1)
                wait(dve, u_ready, e + n)
                at = slice(tiles[0], tiles[-1] + 1)
                dve.reciprocal(rden[:, at, :], den[:, at, :]).then_inc(rden_ready, 1)

            dve.memset(w_up[:], 0.0).then_inc(filled, 1)
            for v in vx:
                last = dve.memset(v[:], 0.0)
            last.then_inc(filled, 1)
            dve.memset(u[:], 0.0)
            dve.memset(power[:], -0.5).then_inc(filled, 1)
            dve.wait_ge(filled, 3)
            for v in vx:
                last = dve.memset(v[:, :, :, DK:DK + 1], 1.0)
            last.then_inc(filled, 1)
            dve.wait_ge(first_loaded, N_FIRST)
            dve.tensor_tensor(bq_even[:], cols[:, COL_BQ:COL_BQ + 1], cols[:, COL_ME:COL_ME + 1], ALU.mult)
            dve.tensor_tensor(bq_odd[:], cols[:, COL_BQ:COL_BQ + 1], cols[:, COL_MO:COL_MO + 1],
                              ALU.mult).then_inc(filled, 1)

            def step(g, G):
                f, e = g - 2, g - 3
                work = []
                for what, has_it, group, t, k in (
                        (second_topk, has(G - 3), e, 2, 8), (first_topk, has(G - 2), f, 0, 6),
                        (first_topk, has(G - 2), f, 1, 6), (second_topk, has(G - 2), f, 0, 8),
                        (first_topk, has(G - 2), f, 2, 6), (second_topk, has(G - 2), f, 1, 8)):
                    for i in range(k):
                        work.append([lambda what=what, group=group, t=t, i=i: what(group, t, i)] if has_it else [])

                def put(i, part, *args):
                    work[i].append(lambda: part(*args))

                for i, n in zip((1, 9, 13, 13, 22, 26), range(2, 8)):
                    if has(G):
                        put(i, row_max, g, n)
                for i, n in zip((29, 41), range(2)):
                    if has(G + 1):
                        put(i, row_max, g + 1, n)
                if G - 2 == NG - 1:
                    put(40, invert_den, f, *late_parts(G - 2)[0])
                if G - 3 == NG - 1:
                    put(7, last_shift, e, 2)
                    put(7, invert_den, e, *late_parts(G - 3)[1])
                    put(7, last_weigh, e, 2)
                elif has(G - 3):
                    put(20, invert_den, e, 0, range(TILES))
                if has(G - 1):
                    put(5, invert_sums, g - 1, 1)
                if has(G):
                    put(33, invert_sums, g, 0)
                for parts in work:
                    for part in parts:
                        part()

            step.engine = dve
            steps(step)

        @block.gpsimd
        def _(pool):
            tt, ts = nc.gpsimd.tensor_tensor, nc.gpsimd.tensor_scalar

            def layernorm(ready, chain, done, g, squares, v, r, src, dst, n):
                pool.wait_ge(ready, g + 1)
                own_wait(pool, pool_passed)
                ts(v[:], squares[:], 1.0 / DM, EPS, ALU.mult, ALU.add).then_inc(chain, 1)
                pool.wait_ge(chain, 2 * g + 1)
                tt(r[:], v[:], power[0:v.shape[0], 0:n], ALU.pow).then_inc(chain, 1)
                pool.wait_ge(chain, 2 * g + 2)
                tt(dst[:], src[:], r[:].unsqueeze(2).to_broadcast([v.shape[0], n, DM]), ALU.mult).then_inc(done, 1)

            def front_ln(g):
                layernorm(hc_ready, ln1, xn_ready, g, ss, var, rstd, hc, xn, GB)

            def tail_ln(g):
                layernorm(hc2_ready, ln2, xn2_ready, g, ss2, var2, rstd2, hc2, xn2, TILES)

            def sums(f, t):
                pool.wait_ge(best_done, 18 * f + 6 * t + 6)
                wait(pool, top_done, 24 * (f - 1) + 8 * t + 8)
                wait(pool, shifted_ready, TILES * (f - 1) + t + 1)
                wait(pool, weights_exp, TILES * (f - 1) + t + 1)
                rest = [run for run in RUNS if run[0] >= 8]
                for sums_of, starts, runs in ((cand8, ROW0_8, RUNS8), (cand, ROW0, RUNS), (left, ROW0, rest)):
                    for i, n, w in runs:
                        dst = sums_of[:, t, :, starts[i]:starts[i] + n * w].rearrange("p h (n w) -> p h n w", n=n)
                        sx = best[:, t, 0, :, i:i + n].unsqueeze(3).to_broadcast([128, HEADS, n, w])
                        sy = best[:, t, 1, :, 0:w].unsqueeze(2).to_broadcast([128, HEADS, n, w])
                        last = tt(dst, sx, sy, ALU.add)
                last.then_inc(cand_ready, 1)

            def shift(e, t):
                pool.wait_ge(top_done, 24 * e + 8 * t + 8)
                wait(pool, weights_exp, TILES * e)
                tt(shifted[:, t, 0:HEADS * NC].rearrange("p (h c) -> p h c", h=HEADS), cand[:, t, :, :],
                   top[:, t, :, 0:1].to_broadcast([128, HEADS, NC]), ALU.subtract)
                tt(shifted[:, t, HEADS * NC:].rearrange("p (h c) -> p h c", h=HEADS), top[:, t, :, :],
                   top[:, t, :, 0:1].to_broadcast([128, HEADS, TOPK]), ALU.subtract).then_inc(shifted_ready, 1)

            def normalise(g, pair):
                pool.wait_ge(rl_ready, 2 * g + pair + 1)
                if pair == 0:
                    wait(pool, ctxT_ps, g)
                dst = ctx_tok[:, 2 * pair:2 * pair + 2, :].rearrange("p b (h d) -> p (b h) d", d=DK)
                tt(dst, ctx_raw[:, :, 0:DK], rl[:].unsqueeze(2).to_broadcast([NP, 16, DK]),
                   ALU.mult).then_inc(ctx_ready, 1)

            def denominators(e, n, tiles):
                at, base = slice(tiles[0], tiles[-1] + 1), 3 * (e + n)
                pool.wait_ge(weights_exp, TILES * e + tiles[-1] + 1)
                src = expd[:, at, HEADS * NC:].rearrange("p t (h k) -> p t h k", h=HEADS)
                tt(den8[:, at], src[:, :, :, 0:8], src[:, :, :, 8:16], ALU.add).then_inc(den_chain, 1)
                pool.wait_ge(den_chain, base + 1)
                tt(den4[:, at], den8[:, at, :, 0:4], den8[:, at, :, 4:8], ALU.add).then_inc(den_chain, 1)
                pool.wait_ge(den_chain, base + 2)
                tt(den2[:, at], den4[:, at, :, 0:2], den4[:, at, :, 2:4], ALU.add).then_inc(den_chain, 1)
                pool.wait_ge(den_chain, base + 3)
                tt(den[:, at, :], den2[:, at, :, 0], den2[:, at, :, 1], ALU.add).then_inc(den_ready, 1)

            def weights(e, n, tiles):
                at, base, width = slice(tiles[0], tiles[-1] + 1), 5 * (e + n), [128, len(tiles), HEADS, NC]
                tt(wsel[:, at], expd[:, at, 0:HEADS * NC].rearrange("p t (h c) -> p t h c", h=HEADS),
                   taken[:, at], ALU.mult).then_inc(wchain, 1)
                pool.wait_ge(wchain, base + 1)
                pool.wait_ge(rden_ready, e + n + 1)
                tt(wnorm[:, at], wsel[:, at], rden[:, at, :].unsqueeze(3).to_broadcast(width),
                   ALU.mult).then_inc(wchain, 1)

            def weigh(e, n, tiles):
                at, base = slice(tiles[0], tiles[-1] + 1), 5 * (e + n)
                pool.wait_ge(wchain, base + 2)
                tt(wsum4[:, at], wnorm[:, at, 0:4], wnorm[:, at, 4:8], ALU.add).then_inc(wchain, 1)
                pool.wait_ge(wchain, base + 3)
                tt(wsum2[:, at], wsum4[:, at, 0:2], wsum4[:, at, 2:4], ALU.add).then_inc(wchain, 1)
                pool.wait_ge(wchain, base + 4)
                tt(wsum1[:, at], wsum2[:, at, 0], wsum2[:, at, 1], ALU.add).then_inc(wchain, 1)
                pool.wait_ge(wchain, base + 5)
                pool.wait_ge(gel_ready, e + 1)
                wait(pool, uT_ps, e + n)
                tt(u[:, at, 0:NC], wsum1[:, at], gel[:, at], ALU.mult).then_inc(u_ready, 1)

            pool.wait_ge(filled, 5)

            def step(g, G):
                f, e = g - 2, g - 3
                if G - 3 == NG - 1:
                    part = late_parts(G - 3)[1]
                    shift(e, 1)
                    denominators(e, *part)
                    weights(e, *part)
                    weigh(e, *part)
                    return
                late, end = (0, range(TILES)), G - 2 == NG - 1
                part = late_parts(NG - 1)[0]
                for present, part, *args in (
                        (has(G - 3), shift, e, 0),
                        (has(G - 3), shift, e, 1),
                        (has(G - 1), normalise, g - 1, 1),
                        (has(G - 3), shift, e, 2),
                        (has(G + 1), front_ln, g + 1),
                        (has(G - 2), sums, f, 0),
                        (has(G - 1), tail_ln, g - 1),
                        (has(G - 3), denominators, e, *late),
                        (has(G - 3), weights, e, *late),
                        (has(G - 3), weigh, e, *late),
                        (has(G - 2), sums, f, 1),
                        (end, shift, f, 0),
                        (has(G), normalise, g, 0),
                        (has(G - 2), sums, f, 2),
                        (end, denominators, f, *part),
                        (end, weights, f, *part),
                        (end, weigh, f, *part)):
                    if present:
                        part(*args)

            step.engine = pool
            steps(step)


def kernel(x, L0_tok_W, L0_tok_b, L0_attn_Wq, L0_attn_bq, L0_attn_Wk, L0_attn_bk, L0_attn_Wv, L0_attn_bv,
           L0_attn_Wo, L0_attn_bo, L0_ffn_W_q, L0_ffn_keys, L0_ffn_down_embed, L0_ffn_up_embed):
    import numpy as np
    import concourse.bacc as bacc
    from concourse.bass_utils import run_bass_kernel_spmd

    segs = np.asarray(x)[:, :NSEG * STRIDE, :].reshape(NG, GB, NSEG, 2, 128)
    x_dev = np.ascontiguousarray(segs.transpose(0, 4, 1, 3, 2))

    tokW = np.asarray(L0_tok_W).T.reshape(NCH, 128, DM).transpose(1, 0, 2).reshape(128, NCH * DM)
    row = np.arange(128)
    even = (row // DK % 2 == 0).astype(np.float32) * DK ** -0.5
    odd = (row // DK % 2 == 1).astype(np.float32) * DK ** -0.5
    ident = np.eye(128, dtype=np.float32)
    center = (np.eye(DM) - 1.0 / DM).astype(np.float32)
    down = np.asarray(L0_ffn_down_embed)[PAIRS].T
    columns = [np.asarray(v)[:, None] for v in (L0_tok_b, L0_attn_bq, L0_attn_bk, L0_attn_bv, L0_attn_bo, even, odd)]
    wpack = np.ascontiguousarray(np.concatenate(
        [tokW, np.asarray(L0_attn_Wq), np.asarray(L0_attn_Wk), np.asarray(L0_attn_Wv), np.asarray(L0_attn_Wo),
         ident, center, down, *columns], axis=1))

    wq = np.asarray(L0_ffn_W_q).reshape(DM, 2 * HEADS, DKEY).transpose(2, 1, 0).reshape(DKEY, -1)
    keys = np.asarray(L0_ffn_keys).transpose(3, 2, 0, 1).reshape(DKEY, -1)
    qkpack = np.ascontiguousarray(np.concatenate([wq, keys], axis=1))
    up = np.ascontiguousarray(np.asarray(L0_ffn_up_embed)[PAIRS])

    nc = bacc.Bacc("TRN2", target_bir_lowering=False, num_devices=1)
    arrays = {"x_dram": x_dev, "wpack_dram": wpack, "qkpack_dram": qkpack, "up_dram": up}
    args = [nc.dram_tensor(name, a.shape, F32, kind="ExternalInput").ap() for name, a in arrays.items()]
    out = nc.dram_tensor("out_0_dram", (BATCH, NP, DM), F32, kind="ExternalOutput").ap()
    build(nc, *args, out)
    r = run_bass_kernel_spmd(nc, [arrays], core_ids=[0])
    return r.results[0]["out_0_dram"]
```
